# Optimizing a Trainium2 kernel written in Bass

```python
import numpy as np
import jax
import jax.numpy as jnp

def _softmax(x, axis=-1):
    return jax.nn.softmax(x, axis=axis)

def _gelu(x):
    return jax.nn.gelu(x, approximate=True)

def _silu(x):
    return jax.nn.silu(x)

def _sigmoid(x):
    return jax.nn.sigmoid(x)

def _layernorm(x, axis=-1, eps=1e-05):
    m = jnp.mean(x, axis=axis, keepdims=True)
    v = jnp.var(x, axis=axis, keepdims=True)
    return (x - m) / jnp.sqrt(v + eps)

def _scatter_add(tgt, idx, src, axis=0):
    return tgt.at[idx].add(src)

def _segment_sum(src, seg, n):
    return jax.ops.segment_sum(src, seg, n)
kernel_name = 'mk_xattn_seq_d2_seqx_r2_97a2a7'

def setup_inputs(seed: int=0):
    np.random.seed(seed)
    _w = jnp.asarray

    def _rec_inputs():
        import jax
        import jax.numpy as jnp
        _rk = jax.random.key(seed)
        x = -0.0001108 + 0.9999 * jax.random.normal(jax.random.fold_in(_rk, 1), (8, 512, 640), jnp.float32)
        _lenS = 512 - jax.random.randint(jax.random.fold_in(_rk, 7), (8,), 0, max(1, 512 // 4) + 1, jnp.int32)
        _lenS2 = 77 - jax.random.randint(jax.random.fold_in(_rk, 8), (8,), 0, max(1, 77 // 4) + 1, jnp.int32)
        _ctx_2048P = jax.random.normal(jax.random.fold_in(_rk, 11), (8, 16, 1024), jnp.float32)
        _ctx_2048c = jax.random.dirichlet(jax.random.fold_in(_rk, 511), 0.3 * jnp.ones((16,), jnp.float32), (8, 77))
        _ctx_2048t = jnp.einsum('bsk,bkd->bsd', _ctx_2048c, _ctx_2048P)
        _ctx_2048t = _ctx_2048t * jax.lax.rsqrt(jnp.mean(jnp.square(_ctx_2048t)) + 1e-12) * 0.953939
        ctx_2048 = -0.000395056 + 1.00006 * (_ctx_2048t + 0.3 * jax.random.normal(jax.random.fold_in(_rk, 611), (8, 77, 1024), jnp.float32))
        fside_S_0 = jax.random.uniform(jax.random.fold_in(_rk, 12), (512,), jnp.float32, 0.0, 0.999706)
        return (x, ctx_2048, fside_S_0)
    x, ctx_2048, fside_S_0 = _rec_inputs()

    def _L0_xattn_setup():
        import jax, jax.numpy as jnp
        import numpy as np
        NUM_HEADS = 20
        TEXT_LEN = 77
        IP_SCALE = 1.0

        def _attend(q, k, v, sm_scale):
            scores = jnp.einsum('bhsd,bhld->bhsl', q, k) * sm_scale
            probs = jax.nn.softmax(scores, axis=-1)
            return jnp.einsum('bhsl,bhld->bhsd', probs, v)

        def _split_heads(x, h):
            b, s, c = x.shape
            return x.reshape(b, s, h, c // h).transpose(0, 2, 1, 3)

        def _merge_heads(x):
            b, h, s, d = x.shape
            return x.transpose(0, 2, 1, 3).reshape(b, s, h * d)
        key = jax.random.key(seed)
        ks = jax.random.split(key, 8)
        B, S, C, CC, L = (8, 2048, 640, 1024, TEXT_LEN + 4)
        sd_q = 1.0 / np.sqrt(C)
        sd_kv = 1.0 / np.sqrt(CC)
        return {'hidden_states': jax.random.normal(ks[0], (B, S, C), jnp.float32), 'encoder_hidden_states': jax.random.normal(ks[1], (B, L, CC), jnp.float32), 'Wq': jax.random.normal(ks[2], (C, C), jnp.float32) * sd_q, 'Wk': jax.random.normal(ks[3], (C, CC), jnp.float32) * sd_kv, 'Wv': jax.random.normal(ks[4], (C, CC), jnp.float32) * sd_kv, 'Wk_ip': jax.random.normal(ks[5], (C, CC), jnp.float32) * sd_kv, 'Wv_ip': jax.random.normal(ks[6], (C, CC), jnp.float32) * sd_kv, 'Wo': jax.random.normal(ks[7], (C, C), jnp.float32) * sd_q, 'bo': jnp.zeros((C,), jnp.float32)}
    _L0_xattn_all = _L0_xattn_setup()
    _L0_xattn_in = {k: v for k, v in _L0_xattn_all.items() if k in ('Wq', 'Wk', 'Wv', 'Wk_ip', 'Wv_ip', 'Wo', 'bo')}
    del _L0_xattn_all

    def _L1_xattn_setup():
        import jax, jax.numpy as jnp
        import numpy as np
        HEADS = 20
        NUM_TOKENS = 4
        IP_SCALE = 1.0
        SEM_SCALE = 0.5
        RESCALE = 1.0
        EPS = 1e-12

        def _l2norm(x, axis=-1):
            n = jnp.sqrt(jnp.sum(x * x, axis=axis, keepdims=True))
            return x / jnp.maximum(n, EPS)
        key = jax.random.key(seed)
        ks = jax.random.split(key, 10)
        B, S, C = (2, 512, 640)
        T, E = (81, 1024)
        inp = {'hidden_states': jax.random.normal(ks[0], (B, S, C), jnp.float32), 'encoder_hidden_states': jax.random.normal(ks[1], (B, T, E), jnp.float32), 'spatial_mask': jax.random.uniform(ks[2], (S,), jnp.float32), 'W_q': jax.random.normal(ks[3], (C, C), jnp.float32) * C ** (-0.5), 'W_k': jax.random.normal(ks[4], (E, C), jnp.float32) * E ** (-0.5), 'W_v': jax.random.normal(ks[5], (E, C), jnp.float32) * E ** (-0.5), 'W_k_ip': jax.random.normal(ks[6], (E, C), jnp.float32) * E ** (-0.5), 'W_v_ip': jax.random.normal(ks[7], (E, C), jnp.float32) * E ** (-0.5), 'W_out': jax.random.normal(ks[8], (C, C), jnp.float32) * C ** (-0.5), 'b_out': jnp.zeros((C,), jnp.float32)}
        return inp
    _L1_xattn_all = _L1_xattn_setup()
    _L1_xattn_in = {k: v for k, v in _L1_xattn_all.items() if k in ('W_q', 'W_k', 'W_v', 'W_k_ip', 'W_v_ip', 'W_out', 'b_out')}
    del _L1_xattn_all
    return {'x': x, 'ctx_2048': ctx_2048, 'fside_S_0': fside_S_0, 'L0_xattn_Wq': _L0_xattn_in['Wq'], 'L0_xattn_Wk': _L0_xattn_in['Wk'], 'L0_xattn_Wv': _L0_xattn_in['Wv'], 'L0_xattn_Wk_ip': _L0_xattn_in['Wk_ip'], 'L0_xattn_Wv_ip': _L0_xattn_in['Wv_ip'], 'L0_xattn_Wo': _L0_xattn_in['Wo'], 'L0_xattn_bo': _L0_xattn_in['bo'], 'L1_xattn_W_q': _L1_xattn_in['W_q'], 'L1_xattn_W_k': _L1_xattn_in['W_k'], 'L1_xattn_W_v': _L1_xattn_in['W_v'], 'L1_xattn_W_k_ip': _L1_xattn_in['W_k_ip'], 'L1_xattn_W_v_ip': _L1_xattn_in['W_v_ip'], 'L1_xattn_W_out': _L1_xattn_in['W_out'], 'L1_xattn_b_out': _L1_xattn_in['b_out']}

def reference(x, ctx_2048, fside_S_0, L0_xattn_Wq, L0_xattn_Wk, L0_xattn_Wv, L0_xattn_Wk_ip, L0_xattn_Wv_ip, L0_xattn_Wo, L0_xattn_bo, L1_xattn_W_q, L1_xattn_W_k, L1_xattn_W_v, L1_xattn_W_k_ip, L1_xattn_W_v_ip, L1_xattn_W_out, L1_xattn_b_out):
    import jax
    import jax.numpy as jnp

    def _L0_xattn_ref(hidden_states, encoder_hidden_states, Wq, Wk, Wv, Wk_ip, Wv_ip, Wo, bo):
        import jax, jax.numpy as jnp
        import numpy as np
        NUM_HEADS = 20
        TEXT_LEN = 77
        IP_SCALE = 1.0

        def _attend(q, k, v, sm_scale):
            scores = jnp.einsum('bhsd,bhld->bhsl', q, k) * sm_scale
            probs = jax.nn.softmax(scores, axis=-1)
            return jnp.einsum('bhsl,bhld->bhsd', probs, v)

        def _split_heads(x, h):
            b, s, c = x.shape
            return x.reshape(b, s, h, c // h).transpose(0, 2, 1, 3)

        def _merge_heads(x):
            b, h, s, d = x.shape
            return x.transpose(0, 2, 1, 3).reshape(b, s, h * d)
        residual = hidden_states
        B, S, C = hidden_states.shape
        H = NUM_HEADS
        D = C // H
        sm_scale = 1.0 / jnp.sqrt(jnp.asarray(D, hidden_states.dtype))
        text = encoder_hidden_states[:, :TEXT_LEN, :]
        ip = encoder_hidden_states[:, TEXT_LEN:, :]
        q = _split_heads(hidden_states @ Wq.T, H)
        k = _split_heads(text @ Wk.T, H)
        v = _split_heads(text @ Wv.T, H)
        out_text = _merge_heads(_attend(q, k, v, sm_scale))
        k_ip = _split_heads(ip @ Wk_ip.T, H)
        v_ip = _split_heads(ip @ Wv_ip.T, H)
        out_ip = _merge_heads(_attend(q, k_ip, v_ip, sm_scale))
        out = out_text + IP_SCALE * out_ip
        out = out @ Wo.T + bo
        return out + residual

    def _L1_xattn_ref(hidden_states, encoder_hidden_states, spatial_mask, W_q, W_k, W_v, W_k_ip, W_v_ip, W_out, b_out):
        import jax, jax.numpy as jnp
        import numpy as np
        HEADS = 20
        NUM_TOKENS = 4
        IP_SCALE = 1.0
        SEM_SCALE = 0.5
        RESCALE = 1.0
        EPS = 1e-12

        def _l2norm(x, axis=-1):
            n = jnp.sqrt(jnp.sum(x * x, axis=axis, keepdims=True))
            return x / jnp.maximum(n, EPS)
        B, S, C = hidden_states.shape
        H = HEADS
        Dh = C // H
        attn_scale = Dh ** (-0.5)
        residual = hidden_states
        text_ehs = encoder_hidden_states[:, :-NUM_TOKENS]
        ip_ehs = encoder_hidden_states[:, -NUM_TOKENS:]

        def heads(x):
            return x.reshape(B, -1, H, Dh).transpose(0, 2, 1, 3)
        q = heads(hidden_states @ W_q)
        k_t = heads(text_ehs @ W_k)
        v_t = heads(text_ehs @ W_v)
        scores_t = jnp.einsum('bhsd,bhtd->bhst', q, k_t) * attn_scale
        probs_t = jax.nn.softmax(scores_t, axis=-1)
        text_out = jnp.einsum('bhst,bhtd->bhsd', probs_t, v_t)
        text_out = text_out.transpose(0, 2, 1, 3).reshape(B, S, C)
        k_ip = heads(ip_ehs @ W_k_ip)
        v_ip = heads(ip_ehs @ W_v_ip)
        attn_scores = jnp.einsum('bhsd,bhnd->bhsn', q, k_ip) * attn_scale
        qsem = jnp.einsum('bhst,bte->bhse', probs_t, text_ehs)
        qsem = _l2norm(qsem)
        ip_n = _l2norm(ip_ehs)
        sem = jnp.einsum('bhse,bne->bhsn', qsem, ip_n)
        sem = jax.lax.stop_gradient(sem)
        fused = attn_scores + SEM_SCALE * sem
        probs_ip = jax.nn.softmax(fused, axis=-1)
        probs_ip = probs_ip * spatial_mask[None, None, :, None]
        ip_out = jnp.einsum('bhsn,bhnd->bhsd', probs_ip, v_ip)
        ip_out = ip_out.transpose(0, 2, 1, 3).reshape(B, S, C)
        out = text_out + IP_SCALE * ip_out
        out = out @ W_out + b_out
        out = out + residual
        return out / RESCALE
    x = _L0_xattn_ref(x, ctx_2048, L0_xattn_Wq, L0_xattn_Wk, L0_xattn_Wv, L0_xattn_Wk_ip, L0_xattn_Wv_ip, L0_xattn_Wo, L0_xattn_bo)
    x = _L1_xattn_ref(x, ctx_2048, fside_S_0, L1_xattn_W_q, L1_xattn_W_k, L1_xattn_W_v, L1_xattn_W_k_ip, L1_xattn_W_v_ip, L1_xattn_W_out, L1_xattn_b_out)
    return x

_drawn_inputs = setup_inputs


def setup_inputs(seed=0):
    import zlib

    import numpy as np

    out = dict(_drawn_inputs(seed))
    spreads = {'L0_xattn_bo': (0.0, 0.1), 'L1_xattn_b_out': (0.0, 0.1)}
    factors = {}
    for name, (base, spread) in spreads.items():
        noise = np.random.default_rng([zlib.crc32(name.encode()), seed]).standard_normal(out[name].shape)
        drawn = base * np.exp(spread * noise) if base else spread * noise
        out[name] = jnp.asarray(drawn.astype(out[name].dtype))
    for name, factor in factors.items():
        out[name] = (out[name] * factor).astype(out[name].dtype)
    return out
```

```python
from contextlib import ExitStack

import concourse.bass as bass
from concourse import mybir

F32 = mybir.dt.float32
F32R = mybir.dt.float32r
I32 = mybir.dt.int32
ALU = mybir.AluOpType
ACT = mybir.ActivationFunctionType
AX = mybir.AxisListType

B, S, C, E_CTX, L = 8, 512, 640, 1024, 77
H = 20
D = C // H
P = 128
N_IP = 4
L_TEXT = L - N_IP
KC = C // P
KE = E_CTX // P
NT = S // P
HG = P // D
G = H // HG
GL = HG * L
SCALE = float(D) ** -0.5
SEM_SCALE = 0.5
EPS = 1e-12
WIN = 96
E_PAD = WIN - L + 1
E_ROW = NT * GL + E_PAD
TOK = B * L
SLOTS = 10
RSQRT_MAGIC = 0x5F3759DF - (1 << 22)
NEWTON_STEPS = 3
PASSES = ((0, 0), (0, 1), (1, 0))


def program(nc, xT, ctxT, mask, L0_WqT, L0_WkT, L0_WvT, L0_WoT, L0_bo, L1_Wq, L1_Wk, L1_Wv, L1_Wkip, L1_Wvip,
            L1_Wo, L1_bo, outT):
    x1T = nc.dram_tensor("x1T", (B, C, S), F32, kind="Internal").ap()
    keys = [nc.dram_tensor(f"keys{i}", (B, P, 2, G, L), F32, kind="Internal").ap() for i in range(2)]
    values = [nc.dram_tensor(f"values{i}", (TOK, C), F32, kind="Internal").ap() for i in range(2)]
    values_ip = nc.dram_tensor("values_ip", (B * N_IP, C), F32, kind="Internal").ap()
    gram = nc.dram_tensor("gram", (B, L, L), F32, kind="Internal").ap()
    context_block(nc, ctxT, [L0_WkT, L0_WvT, L1_Wkip, L1_Wvip, L1_Wk, L1_Wv], keys, values, values_ip, gram)
    layer_block(nc, 0, xT, x1T, L0_WqT, L0_WoT, L0_bo, keys[0], values[0])
    layer_block(nc, 1, x1T, outT, L1_Wq, L1_Wo, L1_bo, keys[1], values[1], mask, values_ip, gram)


def context_block(nc, ctxT, weights, keys, values, values_ip, gram):
    K0, V0, KIP, VIP, K1, V1 = range(6)
    JOBS = 6
    TB = -(-TOK // P)
    NB_H = B // 2
    HALF = NB_H * L
    CH = C // 2
    NIP = B * N_IP

    with ExitStack() as ctx:
        sb = lambda name, shape, dt=F32: ctx.enter_context(nc.sbuf_tensor(name, shape, dt))
        ps = lambda name, shape: ctx.enter_context(nc.psum_tensor(name, shape, F32))
        sem = lambda name: ctx.enter_context(nc.semaphore(name))

        craw = sb("craw", [P, KE, TOK])
        chl = sb("chl", [P, 2, KE, TOK], F32R)
        cip = sb("cip", [P, 2, KE, NIP], F32R)
        cipsq = sb("cipsq", [P, KE, NIP])
        wraw = sb("wraw", [P, KE, C])
        whl = [sb(f"whl{i}", [P, 2, KE, C], F32R) for i in range(2)]
        kst = [sb(f"kst{i}", [P, 2, HALF], F32R) for i in range(2)]
        vst = [sb(f"vst{i}", [P, C]) for i in range(2)]
        kip = sb("kip", [NIP, C])
        kipT = sb("kipT", [P, 2, G, NIP], F32R)
        gst = sb("gst", [L, B, L])
        ripn = sb("ripn", [P, NIP])
        nhalf = sb("nhalf", [P, NIP])
        ones = sb("ones", [P, P])
        ident = sb("ident", [NIP, NIP])

        kps = [ps(f"kps{i}", [P, 512]) for i in range(2)]
        vps = [ps(f"vps{i}", [P, 2, 512]) for i in range(2)]
        mps = [ps(f"mps{i}", [P, 512]) for i in range(2)]

        ctx_in = sem("ctx_in")
        w_in = sem("w_in")
        c_hi = sem("c_hi")
        c_lo = sem("c_lo")
        w_hi = sem("w_hi")
        w_lo = sem("w_lo")
        consts = sem("consts")
        zeroed = sem("zeroed")
        sq_done = sem("sq_done")
        k_ps = sem("k_ps")
        k_hi = sem("k_hi")
        k_lo = sem("k_lo")
        k_out = [sem(f"k_out{i}") for i in range(2)]
        v_ps = sem("v_ps")
        v_cp0 = sem("v_cp0")
        v_cp1 = sem("v_cp1")
        v_out = [sem(f"v_out{i}") for i in range(2)]
        kip_cp = sem("kip_cp")
        kipT_ps = sem("kipT_ps")
        kipT_hi = sem("kipT_hi")
        kipT_lo = sem("kipT_lo")
        norm_ps = sem("norm_ps")
        norm_mx = sem("norm_mx")
        norm_r = sem("norm_r")
        g_ps = sem("g_ps")
        g_cp = sem("g_cp")
        g_sc = sem("g_sc")
        g_out = sem("g_out")

        kunits = [(j, m, h) for j in (K0, K1) for m in range(G) for h in range(2)]
        vunits = [(V0, t) for t in range(TB)] + [(KIP, 0), (VIP, 0)] + [(V1, t) for t in range(TB)]
        kindex = {u: i for i, u in enumerate(kunits)}
        vindex = {u: i for i, u in enumerate(vunits)}
        vstored = [u for u in vunits if u[0] != KIP]
        freed = {KIP: (k_ps, 2 * G), VIP: (v_ps, TB), K1: (v_ps, TB + 1), V1: (v_ps, TB + 2)}
        rows_of = lambda j, t: NIP if j in (KIP, VIP) else min(P, TOK - t * P)

        block = ctx.enter_context(nc.Block())

        @block.gpsimd
        def _(pool):
            pool.dma_start(craw[:], ctxT.rearrange("(k p) t -> p k t", p=P)).then_inc(ctx_in, 16)
            nc.gpsimd.memset(ones[:], 1.0).then_inc(consts, 1)
            nc.gpsimd.memset(nhalf[:], -0.5).then_inc(consts, 1)
            nc.gpsimd.memset(ident[:], 0.0).then_inc(zeroed, 1)
            pool.wait_ge(zeroed, 1)
            nc.gpsimd.affine_select(out=ident[:], in_=ident[:], compare_op=ALU.not_equal, fill=1.0, base=0,
                                    pattern=[[-1, NIP]], channel_multiplier=1).then_inc(consts, 1)
            for j in range(JOBS):
                if j >= 1:
                    pool.wait_ge(w_hi, j)
                    pool.wait_ge(w_lo, j)
                pool.dma_start(wraw[:], weights[j].rearrange("(k p) c -> p k c", p=P)).then_inc(w_in, 16)
                if j == VIP:
                    pool.wait_ge(norm_mx, 1)
                    nc.gpsimd.tensor_tensor(ripn[:], ripn[:], nhalf[:], ALU.pow).then_inc(norm_r, 1)

        @block.sync
        def _(sp):
            def store_k(u):
                i = kindex[u]
                j, m, h = u
                sp.wait_ge(k_lo, i + 1)
                sp.wait_ge(k_hi, i + 1)
                for hl in range(2):
                    sp.dma_start(keys[0 if j == K0 else 1][h * NB_H:(h + 1) * NB_H, :, hl, m, :].rearrange("b p l -> p b l"),
                                 kst[i % 2][:, hl, :].bitcast(F32).rearrange("p (b l) -> p b l", l=L)).then_inc(k_out[i % 2], 16)

            def store_v(u):
                i = vstored.index(u)
                j, t = u
                n = rows_of(j, t)
                sp.wait_ge(v_cp0, vindex[u] + 1)
                sp.wait_ge(v_cp1, vindex[u] + 1)
                dst = values_ip if j == VIP else values[0 if j == V0 else 1][t * P:t * P + n, :]
                sp.dma_start(dst, vst[i % 2][0:n, :]).then_inc(v_out[i % 2], 16)

            for u in kunits[:2 * G]:
                store_k(u)
            for t in range(TB):
                store_v((V0, t))
            sp.wait_ge(g_cp, B)
            sp.wait_ge(g_sc, B)
            sp.dma_start(gram.rearrange("b r l -> r b l"), gst[:]).then_inc(g_out, 16)
            store_v((VIP, 0))
            for u in kunits[2 * G:]:
                store_k(u)
            for t in range(TB):
                store_v((V1, t))
            for r in range(2):
                sp.wait_ge(k_out[r], 32 * (len(kunits) // 2))
                sp.wait_ge(v_out[r], 16 * len(range(r, len(vstored), 2)))
            sp.wait_ge(g_out, 16)

        @block.scalar
        def _(act):
            act.wait_ge(ctx_in, 16)
            nc.scalar.activation(chl[:, 0], craw[:], ACT.Copy).then_inc(c_hi, 1)

            def split_w(j):
                act.wait_ge(w_in, 16 * (j + 1))
                if j in freed:
                    act.wait_ge(*freed[j])
                nc.scalar.activation(whl[j % 2][:, 0], wraw[:], ACT.Copy).then_inc(w_hi, 1)

            def evac_k(u):
                i = kindex[u]
                j, m, h = u
                act.wait_ge(k_ps, i + 1)
                if i >= 2:
                    act.wait_ge(k_out[i % 2], 32 * (i // 2))
                n = L if j == K0 else L_TEXT
                nc.scalar.activation(kst[i % 2][:, 0, :].rearrange("p (b l) -> p b l", l=L)[:, :, 0:n],
                                     kps[i % 2][:, 0:HALF].rearrange("p (b l) -> p b l", l=L)[:, :, 0:n],
                                     ACT.Copy).then_inc(k_hi, 1)

            def evac_v(u):
                i = vindex[u]
                j, t = u
                n = rows_of(j, t)
                act.wait_ge(v_ps, i + 1)
                if j == KIP:
                    dst = kip
                else:
                    si = vstored.index(u)
                    dst = vst[si % 2]
                    if si >= 2:
                        act.wait_ge(v_out[si % 2], 16 * (si // 2))
                nc.scalar.activation(dst[0:n, 0:CH], vps[i % 2][0:n, 0, 0:CH], ACT.Copy).then_inc(v_cp0, 1)

            split_w(K0)
            split_w(V0)
            for u in kunits[:2 * G]:
                evac_k(u)
            split_w(KIP)
            for t in range(TB):
                evac_v((V0, t))
            split_w(VIP)
            for b in range(B):
                act.wait_ge(g_ps, b + 1)
                nc.scalar.activation(gst[:, b, 0:L_TEXT], mps[b % 2][0:L, 0:L_TEXT], ACT.Copy).then_inc(g_cp, 1)
            evac_v((KIP, 0))
            split_w(K1)
            act.wait_ge(kipT_ps, 1)
            nc.scalar.activation(kipT[:, 0], mps[1][:, 0:G * NIP].rearrange("p (g t) -> p g t", t=NIP),
                                 ACT.Copy).then_inc(kipT_hi, 1)
            evac_v((VIP, 0))
            split_w(V1)
            for u in kunits[2 * G:]:
                evac_k(u)
            for t in range(TB):
                evac_v((V1, t))

        @block.vector
        def _(dve):
            dve.wait_ge(c_hi, 1)
            nc.vector.tensor_tensor(chl[:, 1], craw[:], chl[:, 0].bitcast(F32), ALU.subtract).then_inc(c_lo, 1)
            dve.wait_ge(c_lo, 1)
            for hl in range(2):
                src = chl[:, hl].bitcast(F32).rearrange("p k (b l) -> p k b l", l=L)[:, :, :, L_TEXT:L]
                nc.vector.tensor_copy(cip[:, hl].rearrange("p k (b n) -> p k b n", n=N_IP), src).then_inc(sq_done, 1)
            src = craw[:].rearrange("p k (b l) -> p k b l", l=L)[:, :, :, L_TEXT:L]
            nc.vector.tensor_tensor(cipsq[:].rearrange("p k (b n) -> p k b n", n=N_IP), src, src,
                                    ALU.mult).then_inc(sq_done, 1)

            def split_w(j):
                dve.wait_ge(w_hi, j + 1)
                nc.vector.tensor_tensor(whl[j % 2][:, 1], wraw[:], whl[j % 2][:, 0].bitcast(F32),
                                        ALU.subtract).then_inc(w_lo, 1)

            def evac_k(u):
                i = kindex[u]
                j, m, h = u
                n = L if j == K0 else L_TEXT
                dve.wait_ge(k_hi, i + 1)
                view = lambda a: a.rearrange("p (b l) -> p b l", l=L)
                kv = [view(kst[i % 2][:, hl, :]) for hl in range(2)]
                if j == K1:
                    dve.wait_ge(kipT_lo, 1)
                    for hl in range(2):
                        nc.vector.tensor_copy(
                            kv[hl][:, :, L_TEXT:L],
                            kipT[:, hl, m, h * NB_H * N_IP:(h + 1) * NB_H * N_IP].bitcast(F32).rearrange("p (b n) -> p b n", n=N_IP))
                nc.vector.tensor_tensor(kv[1][:, :, 0:n], view(kps[i % 2][:, 0:HALF])[:, :, 0:n],
                                        kv[0][:, :, 0:n].bitcast(F32), ALU.subtract).then_inc(k_lo, 1)

            def evac_v(u):
                i = vindex[u]
                j, t = u
                n = rows_of(j, t)
                dve.wait_ge(v_cp0, i + 1)
                dst = kip if j == KIP else vst[vstored.index(u) % 2]
                nc.vector.tensor_copy(dst[0:n, CH:C], vps[i % 2][0:n, 1, 0:CH]).then_inc(v_cp1, 1)

            split_w(K0)
            split_w(V0)
            for u in kunits[:2 * G]:
                evac_k(u)
            split_w(KIP)
            for t in range(TB):
                evac_v((V0, t))
            split_w(VIP)
            dve.wait_ge(norm_ps, 1)
            nc.vector.tensor_scalar(ripn[:], mps[0][:, 0:NIP], EPS * EPS, None, ALU.max).then_inc(norm_mx, 1)
            dve.wait_ge(norm_r, 1)
            for b in range(B):
                dve.wait_ge(g_cp, b + 1)
                nc.vector.scalar_tensor_tensor(
                    out=gst[:, b, L_TEXT:L], in0=mps[b % 2][0:L, L_TEXT:L], scalar=SEM_SCALE,
                    in1=ripn[0:L, b * N_IP:(b + 1) * N_IP], op0=ALU.mult, op1=ALU.mult).then_inc(g_sc, 1)
            evac_v((KIP, 0))
            split_w(K1)
            dve.wait_ge(kipT_hi, 1)
            nc.vector.tensor_tensor(kipT[:, 1], mps[1][:, 0:G * NIP].rearrange("p (g t) -> p g t", t=NIP),
                                    kipT[:, 0].bitcast(F32), ALU.subtract).then_inc(kipT_lo, 1)
            evac_v((VIP, 0))
            split_w(V1)
            for u in kunits[2 * G:]:
                evac_k(u)
            for t in range(TB):
                evac_v((V1, t))

        @block.tensor
        def _(pe):
            def weights_ready(j):
                pe.wait_ge(w_hi, j + 1)
                pe.wait_ge(w_lo, j + 1)

            def key_job(j):
                weights_ready(j)
                for m in range(G):
                    for h in range(2):
                        i = kindex[(j, m, h)]
                        if i >= 2:
                            pe.wait_ge(k_lo, i - 1)
                        for k in range(KE):
                            for a, b in PASSES:
                                mm = nc.tensor.matmul(kps[i % 2][:, 0:HALF], whl[j % 2][:, a, k, m * P:(m + 1) * P],
                                                      chl[:, b, k, h * HALF:(h + 1) * HALF],
                                                      start=(k == 0 and a == b == 0), stop=(k == KE - 1 and a == 1))
                        mm.then_inc(k_ps, 1)

            def value_job(j, source, n_units):
                weights_ready(j)
                for t in range(n_units):
                    i = vindex[(j, t)]
                    n = rows_of(j, t)
                    if i >= 2:
                        pe.wait_ge(v_cp1, i - 1)
                        pe.wait_ge(v_cp0, i - 1)
                    for c in range(2):
                        for k in range(KE):
                            for a, b in PASSES:
                                mm = nc.tensor.matmul(vps[i % 2][0:n, c, 0:CH], source[:, b, k, t * P:t * P + n],
                                                      whl[j % 2][:, a, k, c * CH:(c + 1) * CH],
                                                      start=(k == 0 and a == b == 0), stop=(k == KE - 1 and a == 1))
                    mm.then_inc(v_ps, 1)

            pe.wait_ge(c_hi, 1)
            pe.wait_ge(c_lo, 1)
            key_job(K0)
            pe.wait_ge(sq_done, 3)
            pe.wait_ge(consts, 3)
            for k in range(KE):
                mm = nc.tensor.matmul(mps[0][:, 0:NIP], ones[:], cipsq[:, k, :], start=(k == 0), stop=(k == KE - 1))
            mm.then_inc(norm_ps, 1)
            value_job(V0, chl, TB)
            for b in range(B):
                if b == 0:
                    pe.wait_ge(norm_mx, 1)
                if b >= 2:
                    pe.wait_ge(g_sc, b - 1)
                for k in range(KE):
                    t = craw[:, k, b * L:(b + 1) * L]
                    mm = nc.tensor.matmul(mps[b % 2][0:L, 0:L], t, t, start=(k == 0), stop=(k == KE - 1))
                mm.then_inc(g_ps, 1)
            value_job(KIP, cip, 1)
            pe.wait_ge(v_cp0, vindex[(KIP, 0)] + 1)
            pe.wait_ge(v_cp1, vindex[(KIP, 0)] + 1)
            pe.wait_ge(g_sc, B)
            for m in range(G):
                mm = nc.tensor.transpose(mps[1][:, m * NIP:(m + 1) * NIP], kip[:, m * P:(m + 1) * P], ident[:])
            mm.then_inc(kipT_ps, 1)
            value_job(VIP, cip, 1)
            key_job(K1)
            value_job(V1, chl, TB)



def layer_block(nc, layer, srcT, dstT, wq, wo, bias, keys, values, mask=None, values_ip=None, gram=None):
    IP = layer == 1
    LT = L_TEXT if IP else L
    PV_LAG = 7 if IP else 6
    NEWTON = 4 * NEWTON_STEPS
    row_parts = lambda n: [slice(0, n)] if n == L else [slice(0, n - 1), slice(n - 1, n)]
    PARTS = len(row_parts(LT))

    with ExitStack() as ctx:
        sb = lambda name, shape, dt=F32: ctx.enter_context(nc.sbuf_tensor(f"{name}_{layer}", shape, dt))
        ps = lambda name, shape: ctx.enter_context(nc.psum_tensor(f"{name}_{layer}", shape, F32))
        sem = lambda name: ctx.enter_context(nc.semaphore(f"{name}_{layer}"))

        wq_hl = sb("wq_hl", [P, 2, KC, C], F32R)
        wo_hl = sb("wo_hl", [P, 2, KC, C], F32R)
        x_hl = sb("x_hl", [P, 2, KC, S], F32R)
        q_hl = sb("q_hl", [P, 2, G, S], F32R)
        o_hl = [sb(f"o_hl{i}", [P, 2, G, S], F32R) for i in range(2)]
        key_bd = sb("key_bd", [P, 2, G, GL], F32R)
        val = sb("val", [P, C])
        xraw = [sb(f"xraw{i}", [P, S]) for i in range(2)]
        res = [sb(f"res{i}", [P, S]) for i in range(2)]
        outs = [sb(f"outs{i}", [P, S]) for i in range(2)]
        ident = sb("ident", [P, P])
        bias_c = sb("bias_c", [P, KC])
        row_max = sb("row_max", [P, 2 * HG])
        den = sb("den", [P, 2, 2 * HG])
        if IP:
            val_ip = sb("val_ip", [P, G, P])
            pipT = sb("pipT", [P, S])
            gm = sb("gm", [P, WIN])
            prod = [sb(f"prod{i}", [P, NT, L]) for i in range(2)]
            norm2 = [sb(f"norm2{i}", [P, HG, NT]) for i in range(2)]
            y = [sb(f"y{i}", [P, HG, NT]) for i in range(2)]
            yx = [sb(f"yx{i}", [P, HG, NT]) for i in range(2)]
            three_halves = sb("three_halves", [P, HG, NT])
            att = sb("att", [P, G, NT, HG, N_IP])
            dot = [sb(f"dot{i}", [P, HG, NT, N_IP]) for i in range(2)]
            fused = sb("fused", [P, NT, HG, N_IP])
            ip_max = sb("ip_max", [P, NT, HG])
            ip_den = sb("ip_den", [P, NT, HG])
            pip = sb("pip", [P, NT, HG * N_IP])
            mask_c = sb("mask_c", [P, NT])
        with ExitStack() as early:
            w_raw = [early.enter_context(nc.sbuf_tensor(f"w_raw{i}_{layer}", [P, KC, C], F32)) for i in range(2)]
        e = sb("e", [P, G, E_ROW])
        pT = [sb(f"pT{i}", [P, HG, S]) for i in range(2)]

        proj_ps = [ps(f"proj_ps{i}", [P, S]) for i in range(2)]
        s_ps = ps("s_ps", [P, 2, 512])
        t_ps = ps("t_ps", [P, 2, S])
        o_ps = ps("o_ps", [P, S])
        if IP:
            g_ps = ps("g_ps", [P, NT, WIN])

        w_in = [sem(f"w_in{i}") for i in range(2)]
        small_in = sem("small_in")
        w_hi, w_lo = sem("w_hi"), sem("w_lo")
        zeroed, ident_0, consts = sem("zeroed"), sem("ident_0"), sem("consts")
        x_in = [sem(f"x_in{i}") for i in range(2)]
        res_in = [sem(f"res_in{i}") for i in range(2)]
        out_done = [sem(f"out_done{i}") for i in range(2)]
        key_in = [sem(f"key_in{i}") for i in range(G)]
        val_in = sem("val_in")
        x_hi, x_lo = sem("x_hi"), sem("x_lo")
        qp_ready, op_ready = sem("qp_ready"), sem("op_ready")
        q_hi, q_lo = sem("q_hi"), sem("q_lo")
        s_ready, max_done, sub_done, exp_done = sem("s_ready"), sem("max_done"), sem("sub_done"), sem("exp_done")
        den_done, rden_done, prob_done = sem("den_done"), sem("rden_done"), sem("prob_done")
        t_ready, t_copied = sem("t_ready"), sem("t_copied")
        pv_ready, o_hi, o_lo = sem("pv_ready"), sem("o_hi"), sem("o_lo")
        y_out = sem("y_out")
        if IP:
            att_done = sem("att_done")
            valip_in, gm_in = sem("valip_in"), sem("gm_in")
            g_ready, prod_done, dot_done, norm_done = sem("g_ready"), sem("prod_done"), sem("dot_done"), sem("norm_done")
            seed_step, newton, dotn_done = sem("seed_step"), sem("newton"), sem("dotn_done")
            ip_step, ip_exp, pip_done = sem("ip_step"), sem("ip_exp"), sem("pip_done")
            it_ready, it_copied = sem("it_ready"), sem("it_copied")

        e_v = [e[:, g, 0:NT * GL].rearrange("p (t h l) -> p t h l", t=NT, h=HG) for g in range(G)]
        srcs = srcT.rearrange("b (k p) s -> b k p s", p=P)
        dsts = dstT.rearrange("b (k p) s -> b k p s", p=P)

        def schedule(engine, half):
            half(0, 0, True, False, True)
            with engine.Fori(0, (B - 2) // 2) as pair:
                half(2 * pair + 1, 1, True, True, True)
                half(2 * pair + 2, 0, True, True, True)
            half(B - 1, 1, True, True, False)
            half(B, 0, False, True, False)

        def of(n, parity, cur, prev, slot, lag, count, stride=1):
            for back in range(2):
                i, rest = divmod(slot + SLOTS * back - lag, stride)
                if rest == 0 and 0 <= i < count and (prev if back else cur):
                    return n - back, parity ^ back, i
            return None

        def s_unit(*a):
            return of(*a, lag=1, count=2 * G)

        def t_unit(*a):
            return of(*a, lag=4, count=2 * G)

        def pv_unit(*a):
            return of(*a, lag=PV_LAG, count=G, stride=2)

        def ring_count(n, par, k):
            before = (par * KC + k) // 2 + 1
            return 16 * ((n - par) * KC // 2 + before) if isinstance(n, int) else 8 * KC * (n - par) + 16 * before

        def load_x(sp, n, k, par=0):
            i = n * KC + k
            ring = (par * KC + k) % 2
            if not (isinstance(n, int) and i < 2):
                sp.wait_ge(x_hi, i - 1)
                sp.wait_ge(x_lo, i - 1)
            sp.dma_start(xraw[ring][:], srcs[n, k]).then_inc(x_in[ring], 16)

        def load_res(sp, n, par, c):
            i = n * G + c
            ring = (par * G + c) % 2
            if c >= 2:
                sp.wait_ge(y_out, i - 1)
            sp.dma_start(res[ring][:], srcs[n, c]).then_inc(res_in[ring], 16)

        def store_out(sp, n, par, c):
            i = n * G + c
            ring = (par * G + c) % 2
            sp.wait_ge(y_out, i + 1)
            sp.dma_start(dsts[n, c], outs[ring][:]).then_inc(out_done[ring], 16)

        def load_keys(sp, n, g):
            for j in range(HG):
                rows = slice(j * D, (j + 1) * D)
                sp.dma_start(key_bd[rows, :, g, j * L:(j + 1) * L].bitcast(F32), keys[n, rows, :, g, :]).then_inc(key_in[g], 16)

        def load_gram(sp, n):
            for rows in row_parts(LT):
                sp.dma_start(gm[rows, 0:L], gram[n, rows]).then_inc(gm_in, 16)

        def load_values(sp, n):
            for rows in row_parts(LT):
                sp.dma_start(val[rows, :], values.rearrange("(b l) c -> b l c", l=L)[n, rows]).then_inc(val_in, 16)
            if IP:
                vip = values_ip.rearrange("(b n) (g j d) -> b n g j d", n=N_IP, j=HG, d=D)
                for j in range(HG):
                    sp.dma_start(val_ip[j * N_IP:(j + 1) * N_IP, :, j * D:(j + 1) * D],
                                 vip[n, :, :, j, :]).then_inc(valip_in, 16)

        def pair_view(u):
            n, par, i = u
            g, tp = divmod(i, 2)
            return e_v[g][:, 2 * tp:2 * tp + 2, :, 0:LT]

        def split_x_lo(pool, n, k, par=0):
            i = n * KC + k
            pool.wait_ge(x_hi, i + 1)
            nc.gpsimd.tensor_tensor(x_hl[:, 1, k, :], xraw[(par * KC + k) % 2][:], x_hl[:, 0, k, :].bitcast(F32),
                                    ALU.subtract).then_inc(x_lo, 1)

        def normalise(pool, n, par, i):
            pool.wait_ge(rden_done, 10 * n + i + 1)
            r = den[:, 1, :].rearrange("p (t h) -> p t h", h=HG)
            v = pair_view((n, par, i))
            nc.gpsimd.tensor_tensor(v, v, r.unsqueeze(3).to_broadcast([P, 2, HG, LT]), ALU.mult).then_inc(prob_done, 1)

        def refine_norm(pool, n, par, g):
            two = (par * G + g) % 2
            base = NEWTON * (G * n + g)
            pool.wait_ge(seed_step, 3 * (G * n + g) + 3)
            for step in range(NEWTON_STEPS):
                c = base + 4 * step
                if step:
                    pool.wait_ge(newton, c)
                nc.gpsimd.tensor_tensor(yx[two][:], y[two][:], y[two][:], ALU.mult).then_inc(newton, 1)
                pool.wait_ge(newton, c + 1)
                nc.gpsimd.tensor_tensor(yx[two][:], yx[two][:], norm2[two][:], ALU.mult).then_inc(newton, 1)
                pool.wait_ge(newton, c + 2)
                nc.gpsimd.tensor_tensor(yx[two][:], three_halves[:], yx[two][:], ALU.subtract).then_inc(newton, 1)
                pool.wait_ge(newton, c + 3)
                nc.gpsimd.tensor_tensor(y[two][:], y[two][:], yx[two][:], ALU.mult).then_inc(newton, 1)
            pool.wait_ge(newton, base + NEWTON)
            pool.wait_ge(dot_done, HG * (G * n + g) + HG)
            for h in range(HG):
                last = nc.gpsimd.tensor_tensor(dot[two][:, h], dot[two][:, h], y[two][:, h].unsqueeze(2).to_broadcast([P, NT, N_IP]),
                                               ALU.mult)
            last.then_inc(dotn_done, 1)

        block = ctx.enter_context(nc.Block())

        @block.sync
        def _(sp):
            for i, w in enumerate((wq, wo)):
                sp.dma_start(w_raw[i][:], w.rearrange("(k p) c -> p k c", p=P)).then_inc(w_in[i], 16)
                if i == 0:
                    for k in range(2):
                        load_x(sp, 0, k)
            sp.dma_start(bias_c[:], bias).then_inc(small_in, 16)
            if IP:
                sp.dma_start(mask_c[:], mask).then_inc(small_in, 16)
            sp.wait_ge(zeroed, 4 if IP else 2)
            for g in range(G):
                load_keys(sp, 0, g)
            load_values(sp, 0)
            if IP:
                load_gram(sp, 0)
            for k in range(2, KC):
                load_x(sp, 0, k)

            def half(n, par, cur, prev, more):
                for slot in range(SLOTS):
                    if IP and slot == 4 and prev and cur:
                        sp.wait_ge(g_ready, 20 * n)
                        load_gram(sp, n)
                    if slot in (3, 4) and prev:
                        load_res(sp, n - 1, 1 - par, slot - 3)
                    if slot in (3, 4) and more:
                        load_x(sp, n + 1, slot - 3, 1 - par)
                    if slot == 1 and prev and cur:
                        sp.wait_ge(s_ready, 10 * n)
                        load_keys(sp, n, G - 1)
                    if cur and more and slot in (3, 5, 7, 9):
                        g = (slot - 3) // 2
                        sp.wait_ge(s_ready, 10 * n + 2 * g + 2)
                        load_keys(sp, n + 1, g)
                    if slot == 5 and prev and cur:
                        sp.wait_ge(pv_ready, G * n)
                        load_values(sp, n)
                    if slot >= 5 and more and slot < 8:
                        load_x(sp, n + 1, slot - 3, 1 - par)
                    if slot >= 6 and prev:
                        store_out(sp, n - 1, 1 - par, slot - 6)
                    if slot >= 5 and slot < 8 and prev:
                        load_res(sp, n - 1, 1 - par, slot - 3)
                if prev:
                    store_out(sp, n - 1, 1 - par, G - 1)

            schedule(sp, half)
            for r in range(2):
                sp.wait_ge(out_done[r], 16 * (B * G // 2))

        @block.gpsimd
        def _(pool):
            nc.gpsimd.memset(key_bd[:].bitcast(F32), 0.0).then_inc(zeroed, 1)
            nc.gpsimd.memset(val[:], 0.0).then_inc(zeroed, 1)
            if IP:
                nc.gpsimd.memset(val_ip[:], 0.0).then_inc(zeroed, 1)
                nc.gpsimd.memset(gm[:], 0.0).then_inc(zeroed, 1)
                nc.gpsimd.memset(pipT[:], 0.0).then_inc(consts, 1)
                nc.gpsimd.memset(three_halves[:], 1.5).then_inc(consts, 1)
            nc.gpsimd.memset(ident[:], 0.0).then_inc(ident_0, 1)
            pool.wait_ge(ident_0, 1)
            nc.gpsimd.affine_select(out=ident[:], in_=ident[:], compare_op=ALU.not_equal, fill=1.0, base=0,
                                    pattern=[[-1, P]], channel_multiplier=1).then_inc(consts, 1)
            pool.wait_ge(w_lo, 2)
            nc.gpsimd.memset(e[:], 0.0 if not IP else 1.0).then_inc(consts, 1)
            for k in range(KC):
                split_x_lo(pool, 0, k)

            def half(n, par, cur, prev, more):
                for slot in range(SLOTS):
                    a = (n, par, cur, prev, slot)
                    if IP and (u := of(*a, lag=6, count=G, stride=2)):
                        refine_norm(pool, *u)
                    if u := s_unit(*a):
                        normalise(pool, *u)
                    if slot >= 5 and more:
                        split_x_lo(pool, n + 1, slot - 5, 1 - par)

            schedule(pool, half)

        @block.scalar
        def _(act):
            def split_x_hi(n, k, par=0):
                i = n * KC + k
                ring = (par * KC + k) % 2
                act.wait_ge(x_in[ring], ring_count(n, par, k))
                if k == 0 and not isinstance(n, int) or isinstance(n, int) and n > 0 and k == 0:
                    act.wait_ge(qp_ready, G * n)
                nc.scalar.activation(x_hl[:, 0, k, :], xraw[ring][:], ACT.Copy).then_inc(x_hi, 1)

            for k in range(2):
                split_x_hi(0, k)
            for i, w in enumerate((wq_hl, wo_hl)):
                act.wait_ge(w_in[i], 16)
                nc.scalar.activation(w[:, 0], w_raw[i][:], ACT.Copy).then_inc(w_hi, 1)
            for k in range(2, KC):
                split_x_hi(0, k)

            def half(n, par, cur, prev, more):
                for slot in range(SLOTS):
                    a = (n, par, cur, prev, slot)
                    if IP and (u := of(*a, lag=5, count=2 * G)):
                        copy_dot(*u, 1)
                    if not IP and (u := pv_unit(*a)):
                        evac_o(*u)
                    u = t_unit(*a)
                    if u:
                        m, mp, i = u
                        g, hp = divmod(i, 2)
                        act.wait_ge(t_ready, 10 * m + i + 1)
                        buf = pT[(mp * G + g) % 2]
                        nc.scalar.activation(buf[0:WIN, 2 * hp:2 * hp + 2, :], t_ps[0:WIN], ACT.Copy).then_inc(t_copied, 1)
                    if IP and (v := pv_unit(*a)):
                        vm, _, vg = v
                        act.wait_ge(it_ready, G * vm + vg + 1)
                        nc.scalar.activation(pipT[0:HG * N_IP, :], o_ps[0:HG * N_IP, :], ACT.Copy).then_inc(it_copied, 1)
                    if v := s_unit(*a):
                        m, mp, i = v
                        act.wait_ge(sub_done, 10 * m + i + 1)
                        if IP:
                            g, tp = divmod(i, 2)
                            nc.scalar.activation(att[:, g, 2 * tp:2 * tp + 2],
                                                 s_ps[:, :, 0:GL].rearrange("p b (h l) -> p b h l", l=L)[:, :, :, L_TEXT:L],
                                                 ACT.Copy).then_inc(att_done, 1)
                        nc.scalar.activation(pair_view(v), pair_view(v), ACT.Exp, scale=SCALE).then_inc(exp_done, 1)
                    if IP and (v := pv_unit(*a)):
                        evac_o(*v)
                    if IP and u:
                        copy_dot(*u, 0)
                    if slot < G and cur:
                        act.wait_ge(qp_ready, G * n + slot + 1)
                        nc.scalar.activation(q_hl[:, 0, slot, :], proj_ps[slot % 2][:], ACT.Copy).then_inc(q_hi, 1)
                    if slot >= G and more:
                        split_x_hi(n + 1, slot - G, 1 - par)
                    if IP and (v := of(*a, lag=6, count=G, stride=2)):
                        m, _, g = v
                        act.wait_ge(ip_step, 5 * (G * m + g) + 3)
                        nc.scalar.activation(fused[:], fused[:], ACT.Exp).then_inc(ip_exp, 1)

            def copy_dot(m, mp, i, hh):
                g, hp = divmod(i, 2)
                act.wait_ge(prod_done, 20 * m + 2 * i + hh + 1)
                if hp == 0 and hh == 0 and not (isinstance(m, int) and G * m + g < 2):
                    act.wait_ge(ip_step, 5 * (G * m + g - 2) + 1)
                nc.scalar.activation(dot[(mp * G + g) % 2][:, 2 * hp + hh], prod[hh][:, :, L_TEXT:L], ACT.Copy).then_inc(dot_done, 1)

            def evac_o(m, mp, g):
                act.wait_ge(pv_ready, G * m + g + 1)
                nc.scalar.activation(o_hl[mp][:, 0, g, :], o_ps[:], ACT.Copy).then_inc(o_hi, 1)

            schedule(act, half)

        @block.vector
        def _(dve):
            for i, w in enumerate((wq_hl, wo_hl)):
                dve.wait_ge(w_hi, i + 1)
                nc.vector.tensor_tensor(w[:, 1], w_raw[i][:], w[:, 0].bitcast(F32), ALU.subtract).then_inc(w_lo, 1)
            dve.wait_ge(small_in, 32 if IP else 16)
            dve.wait_ge(consts, 4 if IP else 2)

            def split_o_lo(m, mp, g):
                dve.wait_ge(o_hi, G * m + g + 1)
                nc.vector.tensor_tensor(o_hl[mp][:, 1, g, :], o_ps[:], o_hl[mp][:, 0, g, :].bitcast(F32),
                                        ALU.subtract).then_inc(o_lo, 1)

            def softmax_front(m, mp, i):
                g, tp = divmod(i, 2)
                src = s_ps[:, :, 0:GL].rearrange("p b (h l) -> p b h l", l=L)[:, :, :, 0:LT]
                mx = row_max[:].rearrange("p (t h) -> p t h", h=HG)
                dve.wait_ge(s_ready, 10 * m + i + 1)
                nc.vector.tensor_reduce(mx, src, AX.X, ALU.max).then_inc(max_done, 1)
                dve.wait_ge(max_done, 10 * m + i + 1)
                nc.vector.tensor_tensor(pair_view((m, mp, i)), src, mx.unsqueeze(3).to_broadcast([P, 2, HG, LT]),
                                        ALU.subtract).then_inc(sub_done, 1)

            def key_sums(m, mp, i):
                c = 10 * m + i + 1
                dve.wait_ge(exp_done, c)
                nc.vector.tensor_reduce(den[:, 0, :].rearrange("p (t h) -> p t h", h=HG), pair_view((m, mp, i)),
                                        AX.X, ALU.add).then_inc(den_done, 1)

            def key_sums_inverse(m, mp, i):
                c = 10 * m + i + 1
                if not (isinstance(m, int) and c == 1):
                    dve.wait_ge(prob_done, c - 1)
                dve.wait_ge(den_done, c)
                nc.vector.reciprocal(den[:, 1, :], den[:, 0, :]).then_inc(rden_done, 1)

            def context_norm(m, mp, i, hh):
                g, hp = divmod(i, 2)
                h = 2 * hp + hh
                c = 20 * m + 2 * i + hh + 1
                dve.wait_ge(g_ready, c)
                if hp == 0 and hh == 0 and not (isinstance(m, int) and G * m + g < 2):
                    dve.wait_ge(newton, NEWTON * (G * m + g - 1))
                if not (isinstance(m, int) and c < 3):
                    dve.wait_ge(norm_done, c - 2)
                    dve.wait_ge(dot_done, c - 2)
                nc.vector.tensor_tensor(prod[hh][:], g_ps[:, :, 0:L], e_v[g][:, :, h, :], ALU.mult).then_inc(prod_done, 1)
                dve.wait_ge(prod_done, c)
                nc.vector.tensor_reduce(norm2[(mp * G + g) % 2][:, h, :], prod[hh][:, :, 0:L_TEXT], AX.X, ALU.add).then_inc(norm_done, 1)

            def norm_seed(m, mp, g):
                two = (mp * G + g) % 2
                c = 3 * (G * m + g)
                dve.wait_ge(norm_done, HG * (G * m + g) + HG)
                nc.vector.tensor_scalar(norm2[two][:], norm2[two][:], EPS * EPS, 0.5, ALU.max, ALU.mult).then_inc(seed_step, 1)
                if not (isinstance(m, int) and G * m + g < 2):
                    dve.wait_ge(dotn_done, G * m + g - 1)
                dve.wait_ge(seed_step, c + 1)
                nc.vector.tensor_scalar(y[two][:].bitcast(I32), norm2[two][:].bitcast(I32), 1, None,
                                        ALU.arith_shift_right).then_inc(seed_step, 1)
                dve.wait_ge(seed_step, c + 2)
                nc.vector.tensor_scalar(y[two][:].bitcast(I32), y[two][:].bitcast(I32), -1.0, float(RSQRT_MAGIC),
                                        ALU.mult, ALU.add).then_inc(seed_step, 1)

            def ip_front(m, mp, g):
                two = (mp * G + g) % 2
                c = 5 * (G * m + g)
                dve.wait_ge(dotn_done, G * m + g + 1)
                dve.wait_ge(att_done, 10 * m + 2 * g + 2)
                for t in range(NT):
                    last = nc.vector.scalar_tensor_tensor(out=fused[:, t], in0=att[:, g, t], scalar=SCALE, in1=dot[two][:, :, t, :],
                                                          op0=ALU.mult, op1=ALU.add)
                last.then_inc(ip_step, 1)
                dve.wait_ge(ip_step, c + 1)
                nc.vector.tensor_reduce(ip_max[:], fused[:], AX.X, ALU.max).then_inc(ip_step, 1)
                dve.wait_ge(ip_step, c + 2)
                nc.vector.tensor_tensor(fused[:], fused[:], ip_max[:].unsqueeze(3).to_broadcast([P, NT, HG, N_IP]),
                                        ALU.subtract).then_inc(ip_step, 1)

            def ip_back(m, mp, g):
                c = 5 * (G * m + g)
                k = 2 * (G * m + g)
                dve.wait_ge(ip_exp, G * m + g + 1)
                nc.vector.tensor_reduce(ip_den[:], fused[:], AX.X, ALU.add).then_inc(ip_step, 1)
                dve.wait_ge(ip_step, c + 4)
                nc.vector.reciprocal(ip_den[:], ip_den[:]).then_inc(ip_step, 1)
                dve.wait_ge(ip_step, c + 5)
                nc.vector.tensor_tensor(ip_den[:], ip_den[:], mask_c[:].unsqueeze(2).to_broadcast([P, NT, HG]),
                                        ALU.mult).then_inc(pip_done, 1)
                dve.wait_ge(pip_done, k + 1)
                if not (isinstance(m, int) and m == 0 and g == 0):
                    dve.wait_ge(it_ready, G * m + g)
                nc.vector.tensor_tensor(pip[:].rearrange("p t (h n) -> p t h n", n=N_IP), fused[:],
                                        ip_den[:].unsqueeze(3).to_broadcast([P, NT, HG, N_IP]),
                                        ALU.mult).then_inc(pip_done, 1)

            def half(n, par, cur, prev, more):
                for slot in range(SLOTS):
                    a = (n, par, cur, prev, slot)
                    if IP and (u := of(*a, lag=5, count=2 * G)):
                        context_norm(*u, 1)
                    if IP and (u := of(*a, lag=6, count=G, stride=2)):
                        norm_seed(*u)
                    if u := s_unit(*a):
                        softmax_front(*u)
                    if not IP and (u := pv_unit(*a)):
                        split_o_lo(*u)
                    su = s_unit(*a)
                    if su:
                        key_sums(*su)
                    if IP and (u := t_unit(*a)) and not pv_unit(*a):
                        context_norm(*u, 0)
                    if su:
                        key_sums_inverse(*su)
                    if IP and (u := pv_unit(*a)):
                        split_o_lo(*u)
                        if u := t_unit(*a):
                            context_norm(*u, 0)
                    if IP and (v := of(*a, lag=6, count=G, stride=2)):
                        ip_front(*v)
                    if slot < G and cur:
                        dve.wait_ge(q_hi, G * n + slot + 1)
                        nc.vector.tensor_tensor(q_hl[:, 1, slot, :], proj_ps[slot % 2][:], q_hl[:, 0, slot, :].bitcast(F32),
                                                ALU.subtract).then_inc(q_lo, 1)
                    if slot >= G and prev:
                        m, mp, c = n - 1, 1 - par, slot - G
                        ring = (mp * G + c) % 2
                        dve.wait_ge(op_ready, G * m + c + 1)
                        dve.wait_ge(res_in[ring], ring_count(m, mp, c))
                        if not (isinstance(m, int) and m == 0 and c < 2):
                            dve.wait_ge(out_done[ring], ring_count(m, mp, c) - 16)
                        nc.vector.scalar_tensor_tensor(out=outs[ring][:], in0=proj_ps[slot % 2][:], scalar=bias_c[:, c:c + 1],
                                                       in1=res[ring][:], op0=ALU.add, op1=ALU.add).then_inc(y_out, 1)
                    if IP and (v := of(*a, lag=6, count=G, stride=2)):
                        ip_back(*v)

            schedule(dve, half)

        @block.tensor
        def _(pe):
            pe.wait_ge(consts, 4 if IP else 2)

            def scores(m, mp, i):
                g, tp = divmod(i, 2)
                c = 10 * m + i
                pe.wait_ge(q_lo, G * m + g + 1)
                if tp == 0:
                    pe.wait_ge(key_in[g], 16 * HG * (m + 1))
                if not (isinstance(m, int) and c == 0):
                    pe.wait_ge(att_done if IP else sub_done, c)
                for b in range(2):
                    t = 2 * tp + b
                    for a, w in PASSES:
                        mm = nc.tensor.matmul(s_ps[:, b, 0:GL], q_hl[:, a, g, t * P:(t + 1) * P], key_bd[:, w, g, :],
                                              start=(a == w == 0), stop=(a == 1))
                mm.then_inc(s_ready, 1)

            def transposes(m, mp, i):
                g, hp = divmod(i, 2)
                c = 10 * m + i
                if hp == 0:
                    pe.wait_ge(prob_done, 10 * m + 2 * g + 2)
                if not (isinstance(m, int) and c == 0):
                    pe.wait_ge(t_copied, c)
                for hh in range(2):
                    for t in range(NT):
                        at = t * GL + (2 * hp + hh) * L
                        mm = nc.tensor.transpose(t_ps[0:WIN, hh, t * P:(t + 1) * P], e[:, g, at:at + WIN], ident[:])
                mm.then_inc(t_ready, 1)

            def gram_product(m, mp, i, hh):
                g, hp = divmod(i, 2)
                c = 20 * m + 2 * i + hh
                if hh == 0:
                    pe.wait_ge(t_copied, 10 * m + i + 1)
                    if i == 0:
                        pe.wait_ge(gm_in, 16 * PARTS * (m + 1))
                if not (isinstance(m, int) and c == 0):
                    pe.wait_ge(prod_done, c)
                buf = pT[(mp * G + g) % 2]
                for t in range(NT):
                    mm = nc.tensor.matmul(g_ps[:, t, :], buf[0:WIN, 2 * hp + hh, t * P:(t + 1) * P], gm[0:WIN, :],
                                          start=(t == 0), stop=(t == NT - 1), skip_group_check=True)
                mm.then_inc(g_ready, 1)

            def transpose_ip(m, mp, g):
                pe.wait_ge(pip_done, 2 * (G * m + g) + 2)
                if not (isinstance(m, int) and m == 0 and g == 0):
                    pe.wait_ge(o_lo, G * m + g)
                for t in range(NT):
                    mm = nc.tensor.transpose(o_ps[0:HG * N_IP, t * P:(t + 1) * P], pip[:, t, :], ident[:])
                mm.then_inc(it_ready, 1)

            def values_product(m, mp, g):
                pe.wait_ge(t_copied, 10 * m + 2 * g + 2)
                if g == 0:
                    pe.wait_ge(val_in, 16 * PARTS * (m + 1))
                if IP:
                    if g == 0:
                        pe.wait_ge(valip_in, 16 * HG * (m + 1))
                    pe.wait_ge(it_copied, G * m + g + 1)
                    nc.tensor.matmul(o_ps[:], val_ip[0:WIN, g, :], pipT[0:WIN, :], start=True, stop=False,
                                     skip_group_check=True)
                elif not (isinstance(m, int) and m == 0 and g == 0):
                    pe.wait_ge(o_lo, G * m + g)
                buf = pT[(mp * G + g) % 2]
                for h in range(HG):
                    at = g * P + h * D
                    mm = nc.tensor.matmul(o_ps[h * D:(h + 1) * D, :], val[0:WIN, at:at + D], buf[0:WIN, h, :],
                                          start=not IP, stop=True, tile_position=(0, h * D), skip_group_check=IP)
                mm.then_inc(pv_ready, 1)

            def project(bank, w, rhs, c, ks, k_of=KC):
                for k in ks:
                    for a, b in PASSES:
                        mm = nc.tensor.matmul(bank[:], w[:, a, k, c * P:(c + 1) * P], rhs[:, b, k, :],
                                              start=(k == 0 and a == b == 0), stop=(k == k_of - 1 and a == 1))
                return mm

            def half(n, par, cur, prev, more):
                for slot in range(SLOTS):
                    a = (n, par, cur, prev, slot)
                    pvu = pv_unit(*a)
                    if not IP and pvu:
                        values_product(*pvu)
                    tu = t_unit(*a)
                    if tu:
                        transposes(*tu)
                    if u := s_unit(*a):
                        scores(*u)
                    if IP and pvu:
                        transpose_ip(*pvu)
                    q, o = slot < G and cur, slot >= G and prev
                    bank = proj_ps[slot % 2]
                    if q:
                        if slot == 0:
                            pe.wait_ge(x_lo, KC * (n + 1))
                            if not prev:
                                pe.wait_ge(w_lo, 1)
                        if slot >= 2:
                            pe.wait_ge(q_lo, G * n + slot - 1)
                        args = (bank, wq_hl, x_hl, slot)
                        ready = qp_ready
                    elif o:
                        if slot == G:
                            pe.wait_ge(o_lo, G * n - 1 if IP else G * n)
                            if isinstance(n, int) and n == 1:
                                pe.wait_ge(w_lo, 2)
                        if slot < G + 2:
                            if cur:
                                pe.wait_ge(q_lo, G * n + slot - 1)
                        else:
                            pe.wait_ge(y_out, G * (n - 1) + slot - G - 1)
                        args = (bank, wo_hl, o_hl[1 - par], slot - G)
                        ready = op_ready
                    first = (KC + 1) // 2
                    if q or o:
                        mm = project(*args, range(first))
                    if IP and pvu:
                        values_product(*pvu)
                    if IP and tu:
                        gram_product(*tu, 0)
                    if q or o:
                        if o and slot == G and IP:
                            project(*args, range(first, KC - 1))
                            pe.wait_ge(o_lo, G * n)
                            first = KC - 1
                        project(*args, range(first, KC)).then_inc(ready, 1)
                    if IP and tu:
                        gram_product(*tu, 1)

            schedule(pe, half)


def kernel(**inputs):
    import numpy as np
    import concourse.bacc as bacc
    from concourse.bass_utils import run_bass_kernel_spmd

    a = {k: np.asarray(v) for k, v in inputs.items()}
    arrays = {
        "xT": a["x"].transpose(0, 2, 1),
        "ctxT": a["ctx_2048"].reshape(TOK, E_CTX).T,
        "mask": a["fside_S_0"].reshape(NT, P).T,
        "L0_WqT": a["L0_xattn_Wq"].T,
        "L0_WkT": a["L0_xattn_Wk"].T,
        "L0_WvT": a["L0_xattn_Wv"].T,
        "L0_WoT": a["L0_xattn_Wo"].T,
        "L0_bo": a["L0_xattn_bo"].reshape(KC, P).T,
        "L1_Wq": a["L1_xattn_W_q"],
        "L1_Wk": a["L1_xattn_W_k"],
        "L1_Wv": a["L1_xattn_W_v"],
        "L1_Wkip": a["L1_xattn_W_k_ip"],
        "L1_Wvip": a["L1_xattn_W_v_ip"],
        "L1_Wo": a["L1_xattn_W_out"],
        "L1_bo": a["L1_xattn_b_out"].reshape(KC, P).T,
    }
    arrays = {k: np.ascontiguousarray(v) for k, v in arrays.items()}
    nc = bacc.Bacc("TRN2", target_bir_lowering=False, num_devices=1)
    args = {k: nc.dram_tensor(k, v.shape, mybir.dt.from_np(v.dtype), kind="ExternalInput").ap() for k, v in arrays.items()}
    out = nc.dram_tensor("outT", (B, C, S), F32, kind="ExternalOutput").ap()
    program(nc, outT=out, **args)
    r = run_bass_kernel_spmd(nc, [arrays], core_ids=[0])
    return r.results[0]["outT"].transpose(0, 2, 1)
```

```python
from contextlib import ExitStack

import concourse.bass as bass
from concourse import mybir

F32 = mybir.dt.float32
F32R = mybir.dt.float32r
I32 = mybir.dt.int32
ALU = mybir.AluOpType
ACT = mybir.ActivationFunctionType
AX = mybir.AxisListType

B, S, C, E_CTX, L = 8, 512, 640, 1024, 77
H = 20
D = C // H
P = 128
N_IP = 4
L_TEXT = L - N_IP
KC = C // P
KE = E_CTX // P
NT = S // P
HG = P // D
G = H // HG
GL = HG * L
SCALE = float(D) ** -0.5
SEM_SCALE = 0.5
EPS = 1e-12
WIN = 96
E_PAD = WIN - L + 1
E_ROW = NT * GL + E_PAD
TOK = B * L
SLOTS = 10
RSQRT_MAGIC = 0x5F3759DF - (1 << 22)
NEWTON_STEPS = 3
PASSES = ((0, 0), (0, 1), (1, 0))


def program(nc, xT, ctxT, mask, L0_WqT, L0_WkT, L0_WvT, L0_WoT, L0_bo, L1_Wq, L1_Wk, L1_Wv, L1_Wkip, L1_Wvip,
            L1_Wo, L1_bo, outT):
    x1T = nc.dram_tensor("x1T", (B, C, S), F32, kind="Internal").ap()
    keys = [nc.dram_tensor(f"keys{i}", (B, P, 2, G, L), F32, kind="Internal").ap() for i in range(2)]
    values = [nc.dram_tensor(f"values{i}", (TOK, C), F32, kind="Internal").ap() for i in range(2)]
    values_ip = nc.dram_tensor("values_ip", (B * N_IP, C), F32, kind="Internal").ap()
    gram = nc.dram_tensor("gram", (B, L, L), F32, kind="Internal").ap()
    split_weights = [nc.dram_tensor(f"split_weights{i}", (P, 2, KC, C), F32, kind="Internal").ap() for i in range(2)]
    with ExitStack() as ctx:
        sb = lambda name, shape, dt: ctx.enter_context(nc.sbuf_tensor(name, shape, dt))
        wq_hl = sb("wq_hl", [P, 2, KC, C], F32R)
        wo_hl = sb("wo_hl", [P, 2, KC, C], F32R)
        with ExitStack() as early:
            craw = early.enter_context(nc.sbuf_tensor("craw", [P, KE, TOK], F32))
        x_hl = sb("x_hl", [P, 2, KC, S], F32R)
        context_block(nc, ctxT, [L0_WkT, L0_WvT, L1_Wkip, L1_Wvip, L1_Wk, L1_Wv],
                      {"wq0": L0_WqT, "wo0": L0_WoT, "wq1": L1_Wq, "wo1": L1_Wo}, xT[0], keys, values, values_ip, gram,
                      split_weights, wq_hl, wo_hl, x_hl, craw)
        attention_block(nc, [xT, x1T, outT], split_weights, [L0_bo, L1_bo], keys, values, mask, values_ip, gram,
                        wq_hl, wo_hl, x_hl)


def context_block(nc, ctxT, weights, later_weights, x0, keys, values, values_ip, gram, split_weights, wq_hl, wo_hl, x_hl, craw):
    K0, V0, KIP, VIP, K1, V1 = range(6)
    TB = -(-TOK // P)
    NB_H = B // 2
    HALF = NB_H * L
    NIP = B * N_IP
    KM = (G + 1) // 2
    VC = C // 2
    BANKS = 6
    K_RING = 3
    k_chunks = lambda j: [(j, 0, KM * P), (j, KM * P, C - KM * P)]
    v_chunks = lambda j: [(j, 0, VC), (j, VC, VC)]
    (k0a, k0b), (k1a, k1b) = k_chunks(K0), k_chunks(K1)
    (v0a, v0b), (v1a, v1b), (kipa, kipb), (vipa, vipb) = (v_chunks(j) for j in (V0, V1, KIP, VIP))
    chunks = [k0a, k0b, v0a, kipa, v0b, kipb, vipa, k1a, vipb, k1b, v1a, v1b]
    WQ1, WO1, X0, WQ0, WO0 = "wq1", "wo1", "x0", "wq0", "wo0"
    beside = {k1a: [WQ1], k1b: [WO1], v1a: [X0], v1b: [WQ0, WO0]}
    loads = [chunks[0]]
    for i, chunk in enumerate(chunks):
        loads += chunks[i + 1:i + 2] + beside.get(chunk, [])
    k_parts = lambda load: ((0, KE // 2), (KE // 2, KE)) if load in chunks else ((0, KC // 2 + 1), (KC // 2 + 1, KC))
    ctx_parts = [(0, 0, KE // 2), (0, KE // 2, KE), (1, 0, KE)]

    with ExitStack() as ctx:
        sb = lambda name, shape, dt=F32: ctx.enter_context(nc.sbuf_tensor(name, shape, dt))
        ps = lambda name, shape: ctx.enter_context(nc.psum_tensor(name, shape, F32))
        sem = lambda name: ctx.enter_context(nc.semaphore(name))

        chl = sb("chl", [P, 2, KE, TOK], F32R)
        cip = sb("cip", [P, 2, KE, NIP], F32R)
        cipsq = sb("cipsq", [P, KE, NIP])
        raw = [sb(f"raw{i}", [P, KC * C]) for i in range(2)]
        whl = [sb(f"whl{i}", [P, 2, KE, KM * P], F32R) for i in range(2)]
        kst = [sb(f"kst{i}", [P, 2, HALF], F32R) for i in range(K_RING)]
        vst = [[sb(f"vst{e}{i}", [P, VC]) for i in range(2)] for e in range(2)]
        kip = sb("kip", [NIP, C])
        kipT = sb("kipT", [P, 2, G, NIP], F32R)
        gst = sb("gst", [L, B, L])
        ripn = sb("ripn", [P, NIP])
        nhalf = sb("nhalf", [P, NIP])
        ones = sb("ones", [P, P])
        ident = sb("ident", [NIP, NIP])

        ups = [ps(f"ups{i}", [P, 512]) for i in range(BANKS)]
        mps = [ps(f"mps{i}", [P, 512]) for i in range(2)]

        ctx_in = [sem(f"ctx_in{i}") for i in range(len(ctx_parts))]
        first_in = [sem(f"first_in{i}") for i in range(2)]
        raw_in = [sem(f"raw_in{i}") for i in range(2)]
        c_hi, c_lo = sem("c_hi"), sem("c_lo")
        w_hi, w_lo = sem("w_hi"), sem("w_lo")
        consts, zeroed = sem("consts"), sem("zeroed")
        sq_done = sem("sq_done")
        u_ps = sem("u_ps")
        k_hi, k_lo = sem("k_hi"), sem("k_lo")
        k_out = [sem(f"k_out{i}") for i in range(K_RING)]
        v_cp = [sem(f"v_cp{e}") for e in range(2)]
        v_out = [[sem(f"v_out{e}{i}") for i in range(2)] for e in range(2)]
        kip_cp = [sem(f"kip_cp{e}") for e in range(2)]
        kipT_ps, kipT_hi, kipT_lo = sem("kipT_ps"), sem("kipT_hi"), sem("kipT_lo")
        norm_ps, norm_mx, norm_r = sem("norm_ps"), sem("norm_mx"), sem("norm_r")
        g_ps, g_cp, g_sc, g_out = sem("g_ps"), sem("g_cp"), sem("g_sc"), sem("g_out")
        w1_out = [sem(f"w1_out{i}") for i in range(2)]

        def units_of(chunk):
            j, c0, n = chunk
            if j in (K0, K1):
                return [(j, m, h) for h in range(2) for m in range(c0 // P, (c0 + n) // P)]
            return [(j, t, c0) for t in range(1 if j in (KIP, VIP) else TB)]

        units = [u for chunk in chunks for u in units_of(chunk)]
        index = {u: i for i, u in enumerate(units)}
        kunits = [u for u in units if u[0] in (K0, K1)]
        vunits = [u for u in units if u[0] in (V0, V1, VIP)]
        kindex = {u: i for i, u in enumerate(kunits)}
        vindex = {u: i for i, u in enumerate(vunits)}
        jobs_end = {chunk: index[units_of(chunk)[-1]] + 1 for chunk in chunks}
        rows_of = lambda j, t: NIP if j in (KIP, VIP) else min(P, TOK - t * P)
        kip_engine = lambda u: 0 if u[2] == 0 else 1

        def read_out(u):
            if u in kindex:
                return k_lo, kindex[u] + 1
            if u[0] == KIP:
                return kip_cp[kip_engine(u)], 1
            return v_cp[vindex[u] % 2], vindex[u] // 2 + 1

        def raw_view(load, q):
            if load in chunks:
                return raw[q % 2][:, 0:KE * load[2]].rearrange("p (k c) -> p k c", k=KE)
            n = S if load == X0 else C
            return raw[q % 2][:, 0:KC * n].rearrange("p (k c) -> p k c", k=KC)

        def split_target(load):
            if load in chunks:
                return whl[chunks.index(load) % 2][:, :, :, 0:load[2]]
            return {WQ1: wq_hl, WO1: wo_hl, X0: x_hl, WQ0: wq_hl, WO0: wo_hl}[load][:]

        block = ctx.enter_context(nc.Block())

        @block.gpsimd
        def _(pool):
            def load(q, what, ks=None):
                if what in chunks:
                    j, c0, n = what
                    src = weights[j][:, c0:c0 + n]
                else:
                    src = x0 if what == X0 else later_weights[what]
                dst, src = raw_view(what, q), src.rearrange("(k p) c -> p k c", p=P)
                return pool.dma_start(dst, src) if ks is None else pool.dma_start(dst[:, ks[0]:ks[1]], src[:, ks[0]:ks[1]])

            def load_ctx(i):
                h, k0, k1 = ctx_parts[i]
                pool.dma_start(craw[:, k0:k1, h * HALF:(h + 1) * HALF],
                               ctxT.rearrange("(k p) t -> p k t", p=P)[:, k0:k1, h * HALF:(h + 1) * HALF]).then_inc(ctx_in[i], 16)

            for i in range(2):
                load(0, loads[0], k_parts(loads[0])[i]).then_inc(first_in[i], 16)
                load_ctx(i)
            load_ctx(2)
            load(1, loads[1]).then_inc(raw_in[1], 16)
            nc.gpsimd.memset(ones[:], 1.0).then_inc(consts, 1)
            nc.gpsimd.memset(nhalf[:], -0.5).then_inc(consts, 1)
            nc.gpsimd.memset(ident[:], 0.0).then_inc(zeroed, 1)
            pool.wait_ge(zeroed, 1)
            nc.gpsimd.affine_select(out=ident[:], in_=ident[:], compare_op=ALU.not_equal, fill=1.0, base=0,
                                    pattern=[[-1, NIP]], channel_multiplier=1).then_inc(consts, 1)
            for q in range(2, len(loads)):
                pool.wait_ge(w_hi, 2 * q - 2)
                pool.wait_ge(w_lo, 2 * q - 2)
                load(q, loads[q]).then_inc(raw_in[q % 2], 16)
                if loads[q] == v0b:
                    pool.wait_ge(norm_mx, 1)
                    nc.gpsimd.tensor_tensor(ripn[:], ripn[:], nhalf[:], ALU.pow).then_inc(norm_r, 1)

        @block.sync
        def _(sp):
            def store_k(u):
                i = kindex[u]
                j, m, h = u
                sp.wait_ge(k_lo, i + 1)
                sp.wait_ge(k_hi, i + 1)
                for hl in range(2):
                    sp.dma_start(keys[0 if j == K0 else 1][h * NB_H:(h + 1) * NB_H, :, hl, m, :].rearrange("b p l -> p b l"),
                                 kst[i % K_RING][:, hl, :].bitcast(F32).rearrange("p (b l) -> p b l", l=L)).then_inc(k_out[i % K_RING], 16)

            def store_v(u):
                e, i = vindex[u] % 2, vindex[u] // 2
                j, t, c0 = u
                n = rows_of(j, t)
                sp.wait_ge(v_cp[e], i + 1)
                dst = values_ip if j == VIP else values[0 if j == V0 else 1][t * P:t * P + n, :]
                sp.dma_start(dst[:, c0:c0 + VC], vst[e][i % 2][0:n, :]).then_inc(v_out[e][i % 2], 16)

            for chunk in chunks:
                for u in units_of(chunk):
                    if u in kindex:
                        store_k(u)
                    elif u in vindex:
                        store_v(u)
                if chunk == kipb:
                    sp.wait_ge(g_cp, B)
                    sp.wait_ge(g_sc, B)
                    sp.dma_start(gram.rearrange("b r l -> r b l"), gst[:]).then_inc(g_out, 16)
                for i, what in enumerate((WQ1, WO1)):
                    if what in beside.get(chunk, []):
                        sp.wait_ge(w_hi, 2 * loads.index(what) + 2)
                        sp.wait_ge(w_lo, 2 * loads.index(what) + 2)
                        sp.dma_start(split_weights[i], (wq_hl, wo_hl)[i][:].bitcast(F32)).then_inc(w1_out[i], 16)
            for r in range(K_RING):
                sp.wait_ge(k_out[r], 32 * len(range(r, len(kunits), K_RING)))
            for e in range(2):
                for r in range(2):
                    sp.wait_ge(v_out[e][r], 16 * len(range(2 * r + e, len(vunits), 4)))
            sp.wait_ge(g_out, 16)
            for i in range(2):
                sp.wait_ge(w1_out[i], 16)

        @block.scalar
        def _(act):
            def split_ctx(i):
                h, k0, k1 = ctx_parts[i]
                at = slice(h * HALF, (h + 1) * HALF)
                act.wait_ge(ctx_in[i], 16)
                nc.scalar.activation(chl[:, 0, k0:k1, at], craw[:, k0:k1, at], ACT.Copy).then_inc(c_hi, 1)

            def split(q, part):
                what = loads[q]
                if q == 0:
                    act.wait_ge(first_in[part], 16)
                elif part == 0:
                    act.wait_ge(raw_in[q % 2], 16 * (q // 2 + q % 2))
                if part == 0 and what in chunks and chunks.index(what) >= 2:
                    act.wait_ge(u_ps, jobs_end[chunks[chunks.index(what) - 2]])
                if part == 0 and what == X0:
                    act.wait_ge(g_ps, B)
                    act.wait_ge(c_lo, len(ctx_parts))
                    act.wait_ge(sq_done, 3)
                if part == 0 and what in (WQ0, WO0):
                    act.wait_ge(w1_out[(WQ0, WO0).index(what)], 16)
                k0, k1 = k_parts(what)[part]
                nc.scalar.activation(split_target(what)[:, 0, k0:k1], raw_view(what, q)[:, k0:k1], ACT.Copy).then_inc(w_hi, 1)

            def evac(u):
                act.wait_ge(u_ps, index[u] + 1)
                bank = ups[index[u] % BANKS]
                j = u[0]
                if u in kindex:
                    i = kindex[u]
                    if i >= K_RING:
                        act.wait_ge(k_out[i % K_RING], 32 * (i // K_RING))
                    n = L if j == K0 else L_TEXT
                    nc.scalar.activation(kst[i % K_RING][:, 0, :].rearrange("p (b l) -> p b l", l=L)[:, :, 0:n],
                                         bank[:, 0:HALF].rearrange("p (b l) -> p b l", l=L)[:, :, 0:n],
                                         ACT.Copy).then_inc(k_hi, 1)
                elif j == KIP:
                    nc.scalar.activation(kip[:, u[2]:u[2] + VC], bank[0:NIP, 0:VC], ACT.Copy).then_inc(kip_cp[0], 1)
                else:
                    i, n = vindex[u] // 2, rows_of(j, u[1])
                    if i >= 2:
                        act.wait_ge(v_out[0][i % 2], 16 * (i // 2))
                    nc.scalar.activation(vst[0][i % 2][0:n, :], bank[0:n, 0:VC], ACT.Copy).then_inc(v_cp[0], 1)

            for i in range(2):
                split(0, i)
                split_ctx(i)
            split_ctx(2)
            for i, chunk in enumerate(chunks):
                for what in chunks[i + 1:i + 2] + beside.get(chunk, []):
                    for part in range(2):
                        split(loads.index(what), part)
                for u in units_of(chunk):
                    if u in kindex or u[0] == KIP and kip_engine(u) == 0 or u in vindex and vindex[u] % 2 == 0:
                        evac(u)
                if chunk == v0b:
                    for b in range(B):
                        act.wait_ge(g_ps, b + 1)
                        nc.scalar.activation(gst[:, b, 0:L_TEXT], mps[b % 2][0:L, 0:L_TEXT], ACT.Copy).then_inc(g_cp, 1)
                if chunk == kipb:
                    act.wait_ge(kipT_ps, 1)
                    nc.scalar.activation(kipT[:, 0], mps[1][:, 0:G * NIP].rearrange("p (g t) -> p g t", t=NIP),
                                         ACT.Copy).then_inc(kipT_hi, 1)

        @block.vector
        def _(dve):
            def split_ctx(i):
                h, k0, k1 = ctx_parts[i]
                at = slice(h * HALF, (h + 1) * HALF)
                dve.wait_ge(c_hi, i + 1)
                nc.vector.tensor_tensor(chl[:, 1, k0:k1, at], craw[:, k0:k1, at], chl[:, 0, k0:k1, at].bitcast(F32),
                                        ALU.subtract).then_inc(c_lo, 1)

            def split(q, part):
                what = loads[q]
                dve.wait_ge(w_hi, 2 * q + part + 1)
                k0, k1 = k_parts(what)[part]
                w = split_target(what)
                nc.vector.tensor_tensor(w[:, 1, k0:k1], raw_view(what, q)[:, k0:k1], w[:, 0, k0:k1].bitcast(F32),
                                        ALU.subtract).then_inc(w_lo, 1)

            def evac(u):
                bank = ups[index[u] % BANKS]
                j = u[0]
                if u in kindex:
                    i = kindex[u]
                    _, m, h = u
                    n = L if j == K0 else L_TEXT
                    dve.wait_ge(k_hi, i + 1)
                    view = lambda a: a.rearrange("p (b l) -> p b l", l=L)
                    kv = [view(kst[i % K_RING][:, hl, :]) for hl in range(2)]
                    if j == K1:
                        dve.wait_ge(kipT_lo, 1)
                        for hl in range(2):
                            nc.vector.tensor_copy(
                                kv[hl][:, :, L_TEXT:L],
                                kipT[:, hl, m, h * NB_H * N_IP:(h + 1) * NB_H * N_IP].bitcast(F32).rearrange("p (b n) -> p b n", n=N_IP))
                    nc.vector.tensor_tensor(kv[1][:, :, 0:n], view(bank[:, 0:HALF])[:, :, 0:n],
                                            kv[0][:, :, 0:n].bitcast(F32), ALU.subtract).then_inc(k_lo, 1)
                    return
                dve.wait_ge(u_ps, index[u] + 1)
                if j == KIP:
                    nc.vector.tensor_copy(kip[:, u[2]:u[2] + VC], bank[0:NIP, 0:VC]).then_inc(kip_cp[1], 1)
                else:
                    i, n = vindex[u] // 2, rows_of(j, u[1])
                    if i >= 2:
                        dve.wait_ge(v_out[1][i % 2], 16 * (i // 2))
                    nc.vector.tensor_copy(vst[1][i % 2][0:n, :], bank[0:n, 0:VC]).then_inc(v_cp[1], 1)

            for i in range(2):
                split(0, i)
                split_ctx(i)
            split_ctx(2)
            for i, chunk in enumerate(chunks):
                for what in chunks[i + 1:i + 2] + beside.get(chunk, []):
                    for part in range(2):
                        split(loads.index(what), part)
                if chunk == k0b:
                    dve.wait_ge(c_lo, len(ctx_parts))
                    for hl in range(2):
                        src = chl[:, hl].bitcast(F32).rearrange("p k (b l) -> p k b l", l=L)[:, :, :, L_TEXT:L]
                        nc.vector.tensor_copy(cip[:, hl].rearrange("p k (b n) -> p k b n", n=N_IP), src).then_inc(sq_done, 1)
                    src = craw[:].rearrange("p k (b l) -> p k b l", l=L)[:, :, :, L_TEXT:L]
                    nc.vector.tensor_tensor(cipsq[:].rearrange("p k (b n) -> p k b n", n=N_IP), src, src,
                                            ALU.mult).then_inc(sq_done, 1)
                for u in units_of(chunk):
                    if u in kindex or u[0] == KIP and kip_engine(u) == 1 or u in vindex and vindex[u] % 2 == 1:
                        evac(u)
                if chunk == k0b:
                    dve.wait_ge(norm_ps, 1)
                    nc.vector.tensor_scalar(ripn[:], mps[0][:, 0:NIP], EPS * EPS, None, ALU.max).then_inc(norm_mx, 1)
                if chunk == v0b:
                    dve.wait_ge(norm_r, 1)
                    for b in range(B):
                        dve.wait_ge(g_cp, b + 1)
                        nc.vector.scalar_tensor_tensor(
                            out=gst[:, b, L_TEXT:L], in0=mps[b % 2][0:L, L_TEXT:L], scalar=SEM_SCALE,
                            in1=ripn[0:L, b * N_IP:(b + 1) * N_IP], op0=ALU.mult, op1=ALU.mult).then_inc(g_sc, 1)
                if chunk == kipb:
                    dve.wait_ge(kipT_hi, 1)
                    nc.vector.tensor_tensor(kipT[:, 1], mps[1][:, 0:G * NIP].rearrange("p (g t) -> p g t", t=NIP),
                                            kipT[:, 0].bitcast(F32), ALU.subtract).then_inc(kipT_lo, 1)

        @block.tensor
        def _(pe):
            for chunk in chunks:
                j, c0, n_cols = chunk
                q, w = loads.index(chunk), whl[chunks.index(chunk) % 2]
                for u in units_of(chunk):
                    i = index[u]
                    bank = ups[i % BANKS]
                    new_chunk = u == units_of(chunk)[0]
                    if i >= BANKS:
                        pe.wait_ge(*read_out(units[i - BANKS]))
                    if chunk == chunks[0] and u[2] == 1 or j == KIP:
                        pe.wait_ge(c_lo, len(ctx_parts))
                    if j == KIP:
                        pe.wait_ge(sq_done, 2)
                    for k in range(KE):
                        if new_chunk and k % (KE // 2) == 0:
                            if q == 0:
                                pe.wait_ge(c_lo, k // (KE // 2) + 1)
                            pe.wait_ge(w_lo, 2 * q + k // (KE // 2) + 1)
                        for a, b in PASSES:
                            flags = dict(start=(k == 0 and a == b == 0), stop=(k == KE - 1 and a == 1))
                            if u in kindex:
                                _, m, h = u
                                mm = nc.tensor.matmul(bank[:, 0:HALF], w[:, a, k, m * P - c0:(m + 1) * P - c0],
                                                      chl[:, b, k, h * HALF:(h + 1) * HALF], **flags)
                            else:
                                source, n = cip if j in (KIP, VIP) else chl, rows_of(j, u[1])
                                mm = nc.tensor.matmul(bank[0:n, 0:VC], source[:, b, k, u[1] * P:u[1] * P + n],
                                                      w[:, a, k, 0:VC], **flags)
                    mm.then_inc(u_ps, 1)
                if chunk == k0b:
                    pe.wait_ge(sq_done, 3)
                    pe.wait_ge(consts, 3)
                    for k in range(KE):
                        mm = nc.tensor.matmul(mps[0][:, 0:NIP], ones[:], cipsq[:, k, :], start=(k == 0), stop=(k == KE - 1))
                    mm.then_inc(norm_ps, 1)
                if chunk == v0b:
                    for b in range(B):
                        if b == 0:
                            pe.wait_ge(norm_mx, 1)
                        if b >= 2:
                            pe.wait_ge(g_sc, b - 1)
                        for k in range(KE):
                            t = craw[:, k, b * L:(b + 1) * L]
                            mm = nc.tensor.matmul(mps[b % 2][0:L, 0:L], t, t, start=(k == 0), stop=(k == KE - 1))
                        mm.then_inc(g_ps, 1)
                if chunk == kipb:
                    for e in range(2):
                        pe.wait_ge(kip_cp[e], 1)
                    pe.wait_ge(g_sc, B)
                    for m in range(G):
                        mm = nc.tensor.transpose(mps[1][:, m * NIP:(m + 1) * NIP], kip[:, m * P:(m + 1) * P], ident[:])
                    mm.then_inc(kipT_ps, 1)


def attention_block(nc, xs, split_weights, bias, keys, values, mask, values_ip, gram, wq_hl, wo_hl, x_hl):
    PV_LAG = (6, 7)
    NEWTON = 4 * NEWTON_STEPS
    keys_of = lambda layer: (L, L_TEXT)[layer]
    row_parts = lambda n: [slice(0, n)] if n == L else [slice(0, n - 1), slice(n - 1, n)]
    PARTS = len(row_parts(L_TEXT))
    with ExitStack() as ctx:
        sb = lambda name, shape, dt=F32: ctx.enter_context(nc.sbuf_tensor(f"a_{name}", shape, dt))
        ps = lambda name, shape: ctx.enter_context(nc.psum_tensor(f"a_{name}", shape, F32))
        sem = lambda name: ctx.enter_context(nc.semaphore(f"a_{name}"))

        q_hl = sb("q_hl", [P, 2, G, S], F32R)
        o_hl = [sb(f"o_hl{i}", [P, 2, G, S], F32R) for i in range(2)]
        key_bd = sb("key_bd", [P, 2, G, GL], F32R)
        val = sb("val", [P, C])
        val_ip = sb("val_ip", [P, G, P])
        xraw = [sb(f"xraw{i}", [P, S]) for i in range(2)]
        res = [sb(f"res{i}", [P, S]) for i in range(2)]
        outs = [sb(f"outs{i}", [P, S]) for i in range(2)]
        ident = sb("ident", [P, P])
        bias_c = sb("bias_c", [P, 2, KC])
        mask_c = sb("mask_c", [P, NT])
        row_max = sb("row_max", [P, 2 * HG])
        den = sb("den", [P, 2, 2 * HG])
        pipT = sb("pipT", [P, S])
        gm = sb("gm", [P, WIN])
        prod = [sb(f"prod{i}", [P, NT, L]) for i in range(2)]
        norm2 = [sb(f"norm2{i}", [P, HG, NT]) for i in range(2)]
        y = [sb(f"y{i}", [P, HG, NT]) for i in range(2)]
        yx = [sb(f"yx{i}", [P, HG, NT]) for i in range(2)]
        three_halves = sb("three_halves", [P, HG, NT])
        att = sb("att", [P, G, NT, HG, N_IP])
        dot = [sb(f"dot{i}", [P, HG, NT, N_IP]) for i in range(2)]
        fused = sb("fused", [P, NT, HG, N_IP])
        ip_max = sb("ip_max", [P, NT, HG])
        ip_den = sb("ip_den", [P, NT, HG])
        pip = sb("pip", [P, NT, HG * N_IP])
        e = sb("e", [P, G, E_ROW])
        pT = [sb(f"pT{i}", [P, HG, S]) for i in range(2)]

        proj_ps = [ps(f"proj_ps{i}", [P, S]) for i in range(2)]
        s_ps = ps("s_ps", [P, 2, 512])
        t_ps = ps("t_ps", [P, 2, S])
        o_ps = ps("o_ps", [P, S])
        g_ps = ps("g_ps", [P, NT, WIN])

        w1_in = [sem(f"w1_in{c}") for c in range(KC)]
        small_in = sem("small_in")
        zeroed, keys_zeroed, ident_0, consts, ones_set = sem("zeroed"), sem("keys_zeroed"), sem("ident_0"), sem("consts"), sem("ones_set")
        x_in = [sem(f"x_in{i}") for i in range(2)]
        res_in = [sem(f"res_in{i}") for i in range(2)]
        out_done = [sem(f"out_done{i}") for i in range(2)]
        key_in = [sem(f"key_in{i}") for i in range(G)]
        val_in = sem("val_in")
        x_hi, x_lo = sem("x_hi"), sem("x_lo")
        qp_ready, op_ready = sem("qp_ready"), sem("op_ready")
        q_hi, q_lo = sem("q_hi"), sem("q_lo")
        s_ready, max_done, sub_done, exp_done = sem("s_ready"), sem("max_done"), sem("sub_done"), sem("exp_done")
        den_done, rden_done, prob_done = sem("den_done"), sem("rden_done"), sem("prob_done")
        t_ready, t_copied = sem("t_ready"), sem("t_copied")
        pv_ready, o_hi, o_lo = sem("pv_ready"), sem("o_hi"), sem("o_lo")
        y_out = sem("y_out")
        att_done = sem("att_done")
        valip_in, gm_in = sem("valip_in"), sem("gm_in")
        g_ready, prod_done, dot_done, norm_done = sem("g_ready"), sem("prod_done"), sem("dot_done"), sem("norm_done")
        seed_step, newton, dotn_done = sem("seed_step"), sem("newton"), sem("dotn_done")
        ip_step, ip_exp, pip_done = sem("ip_step"), sem("ip_exp"), sem("pip_done")
        it_ready, it_copied = sem("it_ready"), sem("it_copied")

        e_v = [e[:, g, 0:NT * GL].rearrange("p (t h l) -> p t h l", t=NT, h=HG) for g in range(G)]
        xs = [x.rearrange("b (k p) s -> b k p s", p=P) for x in xs]

        def schedule(engine, half):
            half(0, 0, 0, None, 0)
            with engine.Fori(0, (B - 2) // 2) as pair:
                half(2 * pair + 1, 1, 0, 0, 0)
                half(2 * pair + 2, 0, 0, 0, 0)
            half(B - 1, 1, 0, 0, 1)
            half(B, 0, 1, 0, 1)
            with engine.Fori(0, (B - 2) // 2) as pair:
                half(2 * pair + B + 1, 1, 1, 1, 1)
                half(2 * pair + B + 2, 0, 1, 1, 1)
            half(2 * B - 1, 1, 1, 1, None)
            half(2 * B, 0, None, 1, None)

        def of(n, parity, cur, prev, slot, lag, count, stride=1, layers=(0, 1)):
            for back in range(2):
                i, rest = divmod(slot + SLOTS * back - lag, stride)
                layer = prev if back else cur
                if rest == 0 and 0 <= i < count and layer in layers:
                    return n - back, parity ^ back, i, layer
            return None

        def s_unit(*a):
            return of(*a, lag=1, count=2 * G)

        def t_unit(*a):
            return of(*a, lag=4, count=2 * G)

        def pv_unit(*a):
            return of(*a, lag=PV_LAG[0], count=G, stride=2, layers=(0,)) or ip_pv_unit(*a)

        def ip_pv_unit(*a):
            return of(*a, lag=PV_LAG[1], count=G, stride=2, layers=(1,))

        def norm_unit(*a):
            return of(*a, lag=6, count=G, stride=2, layers=(1,))

        def first(m, i=0):
            return isinstance(m, int) and m == 0 and i == 0

        def ring_count(m, par, k):
            return 8 * KC * (m - par) + 16 * ((par * KC + k) // 2 + 1)

        def x_count(m, par, k):
            return ring_count(m, par, k) - 16 * ((KC + 1 - (par * KC + k) % 2) // 2)

        def load_x(sp, m, k, layer, par):
            i = (m - 1) * KC + k
            ring = (par * KC + k) % 2
            if layer == 1:
                sp.wait_ge(out_done[ring], ring_count(m - B, par, k) if isinstance(m, int) else 8 * B * G)
            if not (isinstance(m, int) and i < 2):
                sp.wait_ge(x_hi, i - 1)
                sp.wait_ge(x_lo, i - 1)
            sp.dma_start(xraw[ring][:], xs[layer][m - B * layer, k]).then_inc(x_in[ring], 16)

        def load_res(sp, m, par, c, layer):
            ring = (par * G + c) % 2
            if c >= 2:
                sp.wait_ge(y_out, m * G + c - 1)
            sp.dma_start(res[ring][:], xs[layer][m - B * layer, c]).then_inc(res_in[ring], 16)

        def store_out(sp, m, par, c, layer):
            sp.wait_ge(y_out, m * G + c + 1)
            ring = (par * G + c) % 2
            sp.dma_start(xs[layer + 1][m - B * layer, c], outs[ring][:]).then_inc(out_done[ring], 16)

        def load_w1(sp, i, c):
            sp.wait_ge((qp_ready, op_ready)[i], G * (B - 1) + c + 1)
            cols = slice(c * P, (c + 1) * P)
            sp.dma_start((wq_hl, wo_hl)[i][:, :, :, cols].bitcast(F32), split_weights[i][:, :, :, cols]).then_inc(w1_in[c], 16)

        def load_keys(sp, m, g, layer):
            for j in range(HG):
                rows = slice(j * D, (j + 1) * D)
                sp.dma_start(key_bd[rows, :, g, j * L:(j + 1) * L].bitcast(F32),
                             keys[layer][m - B * layer, rows, :, g, :]).then_inc(key_in[g], 16)

        def load_gram(sp, r):
            for rows in row_parts(L_TEXT):
                sp.dma_start(gm[rows, 0:L], gram[r, rows]).then_inc(gm_in, 16)

        def load_values(sp, m, layer):
            b = m - B * layer
            if isinstance(m, int) and m == B:
                sp.dma_start(val[L_TEXT:L, :], val[WIN - N_IP:WIN, :]).then_inc(val_in, 16)
            for rows in row_parts(keys_of(layer)):
                sp.dma_start(val[rows, :], values[layer].rearrange("(b l) c -> b l c", l=L)[b, rows]).then_inc(val_in, 16)
            if layer == 1:
                vip = values_ip.rearrange("(b n) (g j d) -> b n g j d", n=N_IP, j=HG, d=D)
                for j in range(HG):
                    sp.dma_start(val_ip[j * N_IP:(j + 1) * N_IP, :, j * D:(j + 1) * D],
                                 vip[b, :, :, j, :]).then_inc(valip_in, 16)

        def values_count(m, layer):
            return 16 * (m + 1) if layer == 0 else 16 * (B + 1) + 16 * PARTS * (m - B + 1)

        def pair_view(u):
            m, par, i, layer = u
            g, tp = divmod(i, 2)
            return e_v[g][:, 2 * tp:2 * tp + 2, :, 0:keys_of(layer)]

        def split_x_lo(pool, n, k, par):
            i = (n - 1) * KC + k
            pool.wait_ge(x_hi, i + 1)
            nc.gpsimd.tensor_tensor(x_hl[:, 1, k, :], xraw[(par * KC + k) % 2][:], x_hl[:, 0, k, :].bitcast(F32),
                                    ALU.subtract).then_inc(x_lo, 1)

        def normalise(pool, m, par, i, layer):
            pool.wait_ge(rden_done, 10 * m + i + 1)
            r = den[:, 1, :].rearrange("p (t h) -> p t h", h=HG)
            v = pair_view((m, par, i, layer))
            nc.gpsimd.tensor_tensor(v, v, r.unsqueeze(3).to_broadcast([P, 2, HG, keys_of(layer)]), ALU.mult).then_inc(prob_done, 1)

        def refine_norm(pool, m, par, g, layer):
            two = (par * G + g) % 2
            i = G * (m - B) + g
            base = NEWTON * i
            pool.wait_ge(seed_step, 3 * i + 3)
            for step in range(NEWTON_STEPS):
                c = base + 4 * step
                if step:
                    pool.wait_ge(newton, c)
                nc.gpsimd.tensor_tensor(yx[two][:], y[two][:], y[two][:], ALU.mult).then_inc(newton, 1)
                pool.wait_ge(newton, c + 1)
                nc.gpsimd.tensor_tensor(yx[two][:], yx[two][:], norm2[two][:], ALU.mult).then_inc(newton, 1)
                pool.wait_ge(newton, c + 2)
                nc.gpsimd.tensor_tensor(yx[two][:], three_halves[:], yx[two][:], ALU.subtract).then_inc(newton, 1)
                pool.wait_ge(newton, c + 3)
                nc.gpsimd.tensor_tensor(y[two][:], y[two][:], yx[two][:], ALU.mult).then_inc(newton, 1)
            pool.wait_ge(newton, base + NEWTON)
            pool.wait_ge(dot_done, HG * i + HG)
            for h in range(HG):
                last = nc.gpsimd.tensor_tensor(dot[two][:, h], dot[two][:, h], y[two][:, h].unsqueeze(2).to_broadcast([P, NT, N_IP]),
                                               ALU.mult)
            last.then_inc(dotn_done, 1)

        block = ctx.enter_context(nc.Block())

        @block.sync
        def _(sp):
            sp.wait_ge(keys_zeroed, 1)
            for g in range(G):
                load_keys(sp, 0, g, 0)
            sp.wait_ge(zeroed, 3)
            load_values(sp, 0, 0)
            load_gram(sp, 0)
            for layer in range(2):
                sp.dma_start(bias_c[:, layer], bias[layer]).then_inc(small_in, 16)
            sp.dma_start(mask_c[:], mask).then_inc(small_in, 16)

            def half(n, par, cur, prev, nxt):
                has_cur, has_prev, more = cur is not None, prev is not None, nxt is not None
                for slot in range(SLOTS):
                    if slot == 4 and prev == 1 and cur == 1:
                        sp.wait_ge(g_ready, 20 * (n - B))
                        load_gram(sp, n - B)
                    if slot in (3, 4) and has_prev:
                        load_res(sp, n - 1, 1 - par, slot - 3, prev)
                    if slot in (3, 4) and more:
                        load_x(sp, n + 1, slot - 3, nxt, 1 - par)
                    if slot == 1 and has_prev and has_cur:
                        sp.wait_ge(s_ready, 10 * n)
                        load_keys(sp, n, G - 1, cur)
                    if has_cur and more and slot in (3, 5, 7, 9):
                        g = (slot - 3) // 2
                        sp.wait_ge(s_ready, 10 * n + 2 * g + 2)
                        load_keys(sp, n + 1, g, nxt)
                    if slot == 5 and has_prev and has_cur:
                        sp.wait_ge(pv_ready, G * n)
                        load_values(sp, n, cur)
                    if slot >= 5 and more and slot < 8:
                        load_x(sp, n + 1, slot - 3, nxt, 1 - par)
                    if isinstance(n, int) and n == B - 1 and 3 <= slot < 3 + KC:
                        load_w1(sp, 0, slot - 3)
                    if isinstance(n, int) and n == B and slot > G:
                        load_w1(sp, 1, slot - G - 1)
                    if slot >= 6 and has_prev:
                        store_out(sp, n - 1, 1 - par, slot - 6, prev)
                    if slot >= 5 and slot < 8 and has_prev:
                        load_res(sp, n - 1, 1 - par, slot - 3, prev)
                if isinstance(n, int) and n == B:
                    load_w1(sp, 1, KC - 1)
                if has_prev:
                    store_out(sp, n - 1, 1 - par, G - 1, prev)

            schedule(sp, half)
            for r in range(2):
                sp.wait_ge(out_done[r], 16 * (2 * B * G // 2))

        @block.gpsimd
        def _(pool):
            for zeros in (val, val_ip, gm):
                nc.gpsimd.memset(zeros[:], 0.0).then_inc(zeroed, 1)
            nc.gpsimd.memset(pipT[:], 0.0).then_inc(consts, 1)
            nc.gpsimd.memset(three_halves[:], 1.5).then_inc(consts, 1)
            nc.gpsimd.memset(ident[:], 0.0).then_inc(ident_0, 1)
            pool.wait_ge(ident_0, 1)
            nc.gpsimd.affine_select(out=ident[:], in_=ident[:], compare_op=ALU.not_equal, fill=1.0, base=0,
                                    pattern=[[-1, P]], channel_multiplier=1).then_inc(consts, 1)
            nc.gpsimd.memset(e[:, :, NT * GL:E_ROW], 0.0).then_inc(consts, 1)

            def half(n, par, cur, prev, nxt):
                for slot in range(SLOTS):
                    a = (n, par, cur, prev, slot)
                    if u := norm_unit(*a):
                        refine_norm(pool, *u)
                    if u := s_unit(*a):
                        normalise(pool, *u)
                    if (u := of(*a, lag=6, count=G, stride=2, layers=(0,))) and isinstance(u[0], int) and u[0] == B - 1:
                        pool.wait_ge(t_ready, 10 * u[0] + 2 * u[2] + 2)
                        nc.gpsimd.memset(e_v[u[2]][:, :, :, L_TEXT:L], 1.0).then_inc(ones_set, 1)
                    if slot >= 5 and nxt is not None:
                        split_x_lo(pool, n + 1, slot - 5, 1 - par)

            schedule(pool, half)

        @block.scalar
        def _(act):
            def split_x_hi(n, k, par):
                ring = (par * KC + k) % 2
                act.wait_ge(x_in[ring], x_count(n, par, k))
                if k == 0:
                    act.wait_ge(qp_ready, G * n)
                nc.scalar.activation(x_hl[:, 0, k, :], xraw[ring][:], ACT.Copy).then_inc(x_hi, 1)

            def half(n, par, cur, prev, nxt):
                has_cur, has_prev, more = cur is not None, prev is not None, nxt is not None
                for slot in range(SLOTS):
                    a = (n, par, cur, prev, slot)
                    if u := of(*a, lag=5, count=2 * G, layers=(1,)):
                        copy_dot(*u, 1)
                    ipu = ip_pv_unit(*a)
                    if not ipu and (u := pv_unit(*a)):
                        evac_o(*u)
                    u = t_unit(*a)
                    if u:
                        m, mp, i, _ = u
                        g, hp = divmod(i, 2)
                        act.wait_ge(t_ready, 10 * m + i + 1)
                        buf = pT[(mp * G + g) % 2]
                        nc.scalar.activation(buf[0:WIN, 2 * hp:2 * hp + 2, :], t_ps[0:WIN], ACT.Copy).then_inc(t_copied, 1)
                    if ipu:
                        act.wait_ge(it_ready, G * (ipu[0] - B) + ipu[2] + 1)
                        nc.scalar.activation(pipT[0:HG * N_IP, :], o_ps[0:HG * N_IP, :], ACT.Copy).then_inc(it_copied, 1)
                    if v := s_unit(*a):
                        m, mp, i, layer = v
                        act.wait_ge(sub_done, 10 * m + i + 1)
                        if layer == 1:
                            g, tp = divmod(i, 2)
                            nc.scalar.activation(att[:, g, 2 * tp:2 * tp + 2],
                                                 s_ps[:, :, 0:GL].rearrange("p b (h l) -> p b h l", l=L)[:, :, :, L_TEXT:L],
                                                 ACT.Copy).then_inc(att_done, 1)
                        nc.scalar.activation(pair_view(v), pair_view(v), ACT.Exp, scale=SCALE).then_inc(exp_done, 1)
                    if ipu:
                        evac_o(*ipu)
                    if u and u[3] == 1:
                        copy_dot(*u, 0)
                    if slot < G and has_cur:
                        act.wait_ge(qp_ready, G * n + slot + 1)
                        nc.scalar.activation(q_hl[:, 0, slot, :], proj_ps[slot % 2][:], ACT.Copy).then_inc(q_hi, 1)
                    if slot >= G and more:
                        split_x_hi(n + 1, slot - G, 1 - par)
                    if v := norm_unit(*a):
                        m, _, g, _ = v
                        act.wait_ge(ip_step, 5 * (G * (m - B) + g) + 3)
                        nc.scalar.activation(fused[:], fused[:], ACT.Exp).then_inc(ip_exp, 1)

            def copy_dot(m, mp, i, layer, hh):
                g, hp = divmod(i, 2)
                r = m - B
                act.wait_ge(prod_done, 20 * r + 2 * i + hh + 1)
                if hp == 0 and hh == 0 and not (isinstance(r, int) and G * r + g < 2):
                    act.wait_ge(ip_step, 5 * (G * r + g - 2) + 1)
                nc.scalar.activation(dot[(mp * G + g) % 2][:, 2 * hp + hh], prod[hh][:, :, L_TEXT:L], ACT.Copy).then_inc(dot_done, 1)

            def evac_o(m, mp, g, layer):
                act.wait_ge(pv_ready, G * m + g + 1)
                nc.scalar.activation(o_hl[mp][:, 0, g, :], o_ps[:], ACT.Copy).then_inc(o_hi, 1)

            schedule(act, half)

        @block.vector
        def _(dve):
            nc.vector.memset(key_bd[:].bitcast(F32), 0.0).then_inc(keys_zeroed, 1)

            def split_o_lo(m, mp, g, layer):
                dve.wait_ge(o_hi, G * m + g + 1)
                nc.vector.tensor_tensor(o_hl[mp][:, 1, g, :], o_ps[:], o_hl[mp][:, 0, g, :].bitcast(F32),
                                        ALU.subtract).then_inc(o_lo, 1)

            def softmax_front(m, mp, i, layer):
                g, tp = divmod(i, 2)
                LT = keys_of(layer)
                src = s_ps[:, :, 0:GL].rearrange("p b (h l) -> p b h l", l=L)[:, :, :, 0:LT]
                mx = row_max[:].rearrange("p (t h) -> p t h", h=HG)
                dve.wait_ge(s_ready, 10 * m + i + 1)
                nc.vector.tensor_reduce(mx, src, AX.X, ALU.max).then_inc(max_done, 1)
                dve.wait_ge(max_done, 10 * m + i + 1)
                nc.vector.tensor_tensor(pair_view((m, mp, i, layer)), src, mx.unsqueeze(3).to_broadcast([P, 2, HG, LT]),
                                        ALU.subtract).then_inc(sub_done, 1)

            def key_sums(m, mp, i, layer):
                c = 10 * m + i + 1
                dve.wait_ge(exp_done, c)
                nc.vector.tensor_reduce(den[:, 0, :].rearrange("p (t h) -> p t h", h=HG), pair_view((m, mp, i, layer)),
                                        AX.X, ALU.add).then_inc(den_done, 1)

            def key_sums_inverse(m, mp, i, layer):
                c = 10 * m + i + 1
                if not (isinstance(m, int) and c == 1):
                    dve.wait_ge(prob_done, c - 1)
                dve.wait_ge(den_done, c)
                nc.vector.reciprocal(den[:, 1, :], den[:, 0, :]).then_inc(rden_done, 1)

            def context_norm(m, mp, i, layer, hh):
                g, hp = divmod(i, 2)
                h = 2 * hp + hh
                r = m - B
                c = 20 * r + 2 * i + hh + 1
                dve.wait_ge(g_ready, c)
                if hp == 0 and hh == 0 and not (isinstance(r, int) and G * r + g < 2):
                    dve.wait_ge(newton, NEWTON * (G * r + g - 1))
                if not (isinstance(r, int) and c < 3):
                    dve.wait_ge(norm_done, c - 2)
                    dve.wait_ge(dot_done, c - 2)
                nc.vector.tensor_tensor(prod[hh][:], g_ps[:, :, 0:L], e_v[g][:, :, h, :], ALU.mult).then_inc(prod_done, 1)
                dve.wait_ge(prod_done, c)
                nc.vector.tensor_reduce(norm2[(mp * G + g) % 2][:, h, :], prod[hh][:, :, 0:L_TEXT], AX.X, ALU.add).then_inc(norm_done, 1)

            def norm_seed(m, mp, g, layer):
                two = (mp * G + g) % 2
                r = m - B
                c = 3 * (G * r + g)
                dve.wait_ge(norm_done, HG * (G * r + g) + HG)
                nc.vector.tensor_scalar(norm2[two][:], norm2[two][:], EPS * EPS, 0.5, ALU.max, ALU.mult).then_inc(seed_step, 1)
                if not (isinstance(r, int) and G * r + g < 2):
                    dve.wait_ge(dotn_done, G * r + g - 1)
                dve.wait_ge(seed_step, c + 1)
                nc.vector.tensor_scalar(y[two][:].bitcast(I32), norm2[two][:].bitcast(I32), 1, None,
                                        ALU.arith_shift_right).then_inc(seed_step, 1)
                dve.wait_ge(seed_step, c + 2)
                nc.vector.tensor_scalar(y[two][:].bitcast(I32), y[two][:].bitcast(I32), -1.0, float(RSQRT_MAGIC),
                                        ALU.mult, ALU.add).then_inc(seed_step, 1)

            def ip_front(m, mp, g, layer):
                two = (mp * G + g) % 2
                r = m - B
                c = 5 * (G * r + g)
                dve.wait_ge(dotn_done, G * r + g + 1)
                dve.wait_ge(att_done, 10 * r + 2 * g + 2)
                for t in range(NT):
                    last = nc.vector.scalar_tensor_tensor(out=fused[:, t], in0=att[:, g, t], scalar=SCALE, in1=dot[two][:, :, t, :],
                                                          op0=ALU.mult, op1=ALU.add)
                last.then_inc(ip_step, 1)
                dve.wait_ge(ip_step, c + 1)
                nc.vector.tensor_reduce(ip_max[:], fused[:], AX.X, ALU.max).then_inc(ip_step, 1)
                dve.wait_ge(ip_step, c + 2)
                nc.vector.tensor_tensor(fused[:], fused[:], ip_max[:].unsqueeze(3).to_broadcast([P, NT, HG, N_IP]),
                                        ALU.subtract).then_inc(ip_step, 1)

            def ip_back(m, mp, g, layer):
                r = m - B
                c = 5 * (G * r + g)
                k = 2 * (G * r + g)
                dve.wait_ge(ip_exp, G * r + g + 1)
                nc.vector.tensor_reduce(ip_den[:], fused[:], AX.X, ALU.add).then_inc(ip_step, 1)
                dve.wait_ge(ip_step, c + 4)
                nc.vector.reciprocal(ip_den[:], ip_den[:]).then_inc(ip_step, 1)
                dve.wait_ge(ip_step, c + 5)
                nc.vector.tensor_tensor(ip_den[:], ip_den[:], mask_c[:].unsqueeze(2).to_broadcast([P, NT, HG]),
                                        ALU.mult).then_inc(pip_done, 1)
                dve.wait_ge(pip_done, k + 1)
                if not first(r, g):
                    dve.wait_ge(it_ready, G * r + g)
                nc.vector.tensor_tensor(pip[:].rearrange("p t (h n) -> p t h n", n=N_IP), fused[:],
                                        ip_den[:].unsqueeze(3).to_broadcast([P, NT, HG, N_IP]),
                                        ALU.mult).then_inc(pip_done, 1)

            def half(n, par, cur, prev, nxt):
                has_cur, has_prev, more = cur is not None, prev is not None, nxt is not None
                for slot in range(SLOTS):
                    a = (n, par, cur, prev, slot)
                    ipu = ip_pv_unit(*a)
                    if u := of(*a, lag=5, count=2 * G, layers=(1,)):
                        context_norm(*u, 1)
                    if u := norm_unit(*a):
                        norm_seed(*u)
                    su = s_unit(*a)
                    if su:
                        softmax_front(*su)
                    if not ipu and (u := pv_unit(*a)):
                        split_o_lo(*u)
                    if su:
                        key_sums(*su)
                    u = of(*a, lag=4, count=2 * G, layers=(1,))
                    if u and not ipu:
                        context_norm(*u, 0)
                    if su:
                        key_sums_inverse(*su)
                    if ipu:
                        split_o_lo(*ipu)
                        if u:
                            context_norm(*u, 0)
                    if v := norm_unit(*a):
                        ip_front(*v)
                    if slot < G and has_cur:
                        dve.wait_ge(q_hi, G * n + slot + 1)
                        nc.vector.tensor_tensor(q_hl[:, 1, slot, :], proj_ps[slot % 2][:], q_hl[:, 0, slot, :].bitcast(F32),
                                                ALU.subtract).then_inc(q_lo, 1)
                    if slot >= G and has_prev:
                        m, mp, c = n - 1, 1 - par, slot - G
                        ring = (mp * G + c) % 2
                        dve.wait_ge(op_ready, G * m + c + 1)
                        dve.wait_ge(res_in[ring], ring_count(m, mp, c))
                        if isinstance(m, int) and m == 0 and c == 0:
                            dve.wait_ge(small_in, 16 * 3)
                        if not (isinstance(m, int) and m == 0 and c < 2):
                            dve.wait_ge(out_done[ring], ring_count(m, mp, c) - 16)
                        nc.vector.scalar_tensor_tensor(out=outs[ring][:], in0=proj_ps[slot % 2][:],
                                                       scalar=bias_c[:, prev, c:c + 1], in1=res[ring][:], op0=ALU.add, op1=ALU.add).then_inc(y_out, 1)
                    if v := norm_unit(*a):
                        ip_back(*v)

            schedule(dve, half)

        @block.tensor
        def _(pe):

            def scores(m, mp, i, layer):
                g, tp = divmod(i, 2)
                c = 10 * m + i
                pe.wait_ge(q_lo, G * m + g + 1)
                if tp == 0:
                    pe.wait_ge(key_in[g], 16 * HG * (m + 1))
                if layer == 1 and not first(m - B, i):
                    pe.wait_ge(att_done, c - 10 * B)
                elif not first(m, i):
                    pe.wait_ge(sub_done, c)
                for b in range(2):
                    t = 2 * tp + b
                    for a, w in PASSES:
                        mm = nc.tensor.matmul(s_ps[:, b, 0:GL], q_hl[:, a, g, t * P:(t + 1) * P], key_bd[:, w, g, :],
                                              start=(a == w == 0), stop=(a == 1))
                mm.then_inc(s_ready, 1)

            def transposes(m, mp, i, layer):
                g, hp = divmod(i, 2)
                c = 10 * m + i
                if hp == 0:
                    pe.wait_ge(prob_done, 10 * m + 2 * g + 2)
                    if isinstance(m, int) and m == B:
                        pe.wait_ge(ones_set, g + 1 if g < 2 else G)
                if not (isinstance(m, int) and c == 0):
                    pe.wait_ge(t_copied, c)
                if first(m, i):
                    pe.wait_ge(consts, 4)
                for hh in range(2):
                    for t in range(NT):
                        at = t * GL + (2 * hp + hh) * L
                        mm = nc.tensor.transpose(t_ps[0:WIN, hh, t * P:(t + 1) * P], e[:, g, at:at + WIN], ident[:])
                mm.then_inc(t_ready, 1)

            def gram_product(m, mp, i, layer, hh):
                g, hp = divmod(i, 2)
                r = m - B
                c = 20 * r + 2 * i + hh
                if hh == 0:
                    pe.wait_ge(t_copied, 10 * m + i + 1)
                    if i == 0:
                        pe.wait_ge(gm_in, 16 * PARTS * (r + 1))
                if not first(r, c):
                    pe.wait_ge(prod_done, c)
                buf = pT[(mp * G + g) % 2]
                for t in range(NT):
                    mm = nc.tensor.matmul(g_ps[:, t, :], buf[0:WIN, 2 * hp + hh, t * P:(t + 1) * P], gm[0:WIN, :],
                                          start=(t == 0), stop=(t == NT - 1), skip_group_check=True)
                mm.then_inc(g_ready, 1)

            def transpose_ip(m, mp, g, layer):
                pe.wait_ge(pip_done, 2 * (G * (m - B) + g) + 2)
                pe.wait_ge(o_lo, G * m + g)
                for t in range(NT):
                    mm = nc.tensor.transpose(o_ps[0:HG * N_IP, t * P:(t + 1) * P], pip[:, t, :], ident[:])
                mm.then_inc(it_ready, 1)

            def values_product(m, mp, g, layer):
                pe.wait_ge(t_copied, 10 * m + 2 * g + 2)
                if g == 0:
                    pe.wait_ge(val_in, values_count(m, layer))
                if layer == 1:
                    if g == 0:
                        pe.wait_ge(valip_in, 16 * HG * (m - B + 1))
                    pe.wait_ge(it_copied, G * (m - B) + g + 1)
                    nc.tensor.matmul(o_ps[:], val_ip[0:WIN, g, :], pipT[0:WIN, :], start=True, stop=False,
                                     skip_group_check=True)
                elif not first(m, g):
                    pe.wait_ge(o_lo, G * m + g)
                buf = pT[(mp * G + g) % 2]
                for h in range(HG):
                    at = g * P + h * D
                    mm = nc.tensor.matmul(o_ps[h * D:(h + 1) * D, :], val[0:WIN, at:at + D], buf[0:WIN, h, :],
                                          start=layer == 0, stop=True, tile_position=(0, h * D),
                                          skip_group_check=layer == 1)
                mm.then_inc(pv_ready, 1)

            def project(bank, w, rhs, c, ks, k_of=KC):
                for k in ks:
                    for a, b in PASSES:
                        mm = nc.tensor.matmul(bank[:], w[:, a, k, c * P:(c + 1) * P], rhs[:, b, k, :],
                                              start=(k == 0 and a == b == 0), stop=(k == k_of - 1 and a == 1))
                return mm

            def half(n, par, cur, prev, nxt):
                has_cur, has_prev, more = cur is not None, prev is not None, nxt is not None
                for slot in range(SLOTS):
                    a = (n, par, cur, prev, slot)
                    ipu = ip_pv_unit(*a)
                    if not ipu and (u := pv_unit(*a)):
                        values_product(*u)
                    tu = t_unit(*a)
                    gu = tu if tu and tu[3] == 1 else None
                    if tu:
                        transposes(*tu)
                    if u := s_unit(*a):
                        scores(*u)
                    if ipu:
                        transpose_ip(*ipu)
                    q, o = slot < G and has_cur, slot >= G and has_prev
                    bank = proj_ps[slot % 2]
                    if q:
                        if slot == 0:
                            if not first(n):
                                pe.wait_ge(x_lo, KC * n)
                        if isinstance(n, int) and n == B:
                            pe.wait_ge(w1_in[slot], 16)
                        if slot >= 2:
                            pe.wait_ge(q_lo, G * n + slot - 1)
                        args = (bank, wq_hl, x_hl, slot)
                        ready = qp_ready
                    elif o:
                        if slot == G:
                            pe.wait_ge(o_lo, G * n - prev)
                        if slot < G + 2:
                            if has_cur:
                                pe.wait_ge(q_lo, G * n + slot - 1)
                        else:
                            pe.wait_ge(y_out, G * (n - 1) + slot - G - 1)
                        if prev == 1:
                            pe.wait_ge(w1_in[slot - G], 32)
                        args = (bank, wo_hl, o_hl[1 - par], slot - G)
                        ready = op_ready
                    at = (KC + 1) // 2
                    if q or o:
                        project(*args, range(at))
                    if ipu:
                        values_product(*ipu)
                    if gu:
                        gram_product(*gu, 0)
                    if q or o:
                        if o and slot == G and prev == 1:
                            project(*args, range(at, KC - 1))
                            pe.wait_ge(o_lo, G * n)
                            at = KC - 1
                        project(*args, range(at, KC)).then_inc(ready, 1)
                    if gu:
                        gram_product(*gu, 1)

            schedule(pe, half)


def kernel(**inputs):
    import numpy as np
    import concourse.bacc as bacc
    from concourse.bass_utils import run_bass_kernel_spmd

    a = {k: np.asarray(v) for k, v in inputs.items()}
    arrays = {
        "xT": a["x"].transpose(0, 2, 1),
        "ctxT": a["ctx_2048"].reshape(TOK, E_CTX).T,
        "mask": a["fside_S_0"].reshape(NT, P).T,
        "L0_WqT": a["L0_xattn_Wq"].T,
        "L0_WkT": a["L0_xattn_Wk"].T,
        "L0_WvT": a["L0_xattn_Wv"].T,
        "L0_WoT": a["L0_xattn_Wo"].T,
        "L0_bo": a["L0_xattn_bo"].reshape(KC, P).T,
        "L1_Wq": a["L1_xattn_W_q"],
        "L1_Wk": a["L1_xattn_W_k"],
        "L1_Wv": a["L1_xattn_W_v"],
        "L1_Wkip": a["L1_xattn_W_k_ip"],
        "L1_Wvip": a["L1_xattn_W_v_ip"],
        "L1_Wo": a["L1_xattn_W_out"],
        "L1_bo": a["L1_xattn_b_out"].reshape(KC, P).T,
    }
    arrays = {k: np.ascontiguousarray(v) for k, v in arrays.items()}
    nc = bacc.Bacc("TRN2", target_bir_lowering=False, num_devices=1)
    args = {k: nc.dram_tensor(k, v.shape, mybir.dt.from_np(v.dtype), kind="ExternalInput").ap() for k, v in arrays.items()}
    out = nc.dram_tensor("outT", (B, C, S), F32, kind="ExternalOutput").ap()
    program(nc, outT=out, **args)
    r = run_bass_kernel_spmd(nc, [arrays], core_ids=[0])
    return r.results[0]["outT"].transpose(0, 2, 1)
```

```python
from contextlib import ExitStack

import concourse.bass as bass
from concourse import mybir

F32 = mybir.dt.float32
F32R = mybir.dt.float32r
I32 = mybir.dt.int32
ALU = mybir.AluOpType
ACT = mybir.ActivationFunctionType
AX = mybir.AxisListType

B, S, C, E_CTX, L = 8, 512, 640, 1024, 77
H = 20
D = C // H
P = 128
N_IP = 4
L_TEXT = L - N_IP
KC = C // P
KE = E_CTX // P
NT = S // P
HG = P // D
G = H // HG
GL = HG * L
SCALE = float(D) ** -0.5
SEM_SCALE = 0.5
EPS = 1e-12
WIN = 96
WIN_IP = WIN + HG * N_IP
E_PAD = WIN - L + 1
E_ROW = NT * GL + E_PAD
TOK = B * L
SLOTS = 10
RSQRT_MAGIC = 0x5F3759DF - (1 << 22)
NEWTON_STEPS = 3
PASSES = ((0, 0), (0, 1), (1, 0))


def program(nc, xT, ctxT, mask, L0_WqT, L0_WkT, L0_WvT, L0_WoT, L0_bo, L1_Wq, L1_Wk, L1_Wv, L1_Wkip, L1_Wvip,
            L1_Wo, L1_bo, outT):
    x1T = nc.dram_tensor("x1T", (B, C, S), F32, kind="Internal").ap()
    keys = [nc.dram_tensor(f"keys{i}", (B, P, 2, G, L), F32, kind="Internal").ap() for i in range(2)]
    values = [nc.dram_tensor(f"values{i}", (TOK, C), F32, kind="Internal").ap() for i in range(2)]
    values_ip = nc.dram_tensor("values_ip", (B * N_IP, C), F32, kind="Internal").ap()
    gram = nc.dram_tensor("gram", (B, L, L), F32, kind="Internal").ap()
    split_weights = [nc.dram_tensor(f"split_weights{i}", (P, 2, KC, C), F32, kind="Internal").ap() for i in range(2)]
    with ExitStack() as ctx:
        sb = lambda name, shape, dt: ctx.enter_context(nc.sbuf_tensor(name, shape, dt))
        wq_hl = sb("wq_hl", [P, 2, KC, C], F32R)
        wo_hl = sb("wo_hl", [P, 2, KC, C], F32R)
        with ExitStack() as early:
            craw = early.enter_context(nc.sbuf_tensor("craw", [P, KE, TOK], F32))
        x_hl = sb("x_hl", [P, 2, KC, S], F32R)
        context_block(nc, ctxT, [L0_WkT, L0_WvT, L1_Wkip, L1_Wvip, L1_Wk, L1_Wv],
                      {"wq0": L0_WqT, "wo0": L0_WoT, "wq1": L1_Wq, "wo1": L1_Wo}, xT[0], keys, values, values_ip, gram,
                      split_weights, wq_hl, wo_hl, x_hl, craw)
        attention_block(nc, [xT, x1T, outT], split_weights, [L0_bo, L1_bo], keys, values, mask, values_ip, gram,
                        wq_hl, wo_hl, x_hl)


def context_block(nc, ctxT, weights, later_weights, x0, keys, values, values_ip, gram, split_weights, wq_hl, wo_hl, x_hl, craw):
    K0, V0, KIP, VIP, K1, V1 = range(6)
    TB = -(-TOK // P)
    NB_H = B // 2
    HALF = NB_H * L
    NIP = B * N_IP
    KM = (G + 1) // 2
    VC = C // 2
    BANKS = 6
    K_RING = 3
    k_chunks = lambda j: [(j, 0, KM * P), (j, KM * P, C - KM * P)]
    v_chunks = lambda j: [(j, 0, VC), (j, VC, VC)]
    (k0a, k0b), (k1a, k1b) = k_chunks(K0), k_chunks(K1)
    (v0a, v0b), (v1a, v1b), (kipa, kipb), (vipa, vipb) = (v_chunks(j) for j in (V0, V1, KIP, VIP))
    chunks = [k0a, k0b, v0a, kipa, v0b, kipb, vipa, k1a, vipb, k1b, v1a, v1b]
    WQ1, WO1, X0, WQ0, WO0 = "wq1", "wo1", "x0", "wq0", "wo0"
    beside = {v0a: [WQ1], k1a: [WO1, X0], k1b: [WQ0], v1a: [WO0]}
    loads = [chunks[0]]
    for i, chunk in enumerate(chunks):
        loads += chunks[i + 1:i + 2] + beside.get(chunk, [])
    PARTS = 4
    KP = KE // PARTS
    k_parts = lambda load: [(i, i + KP) for i in range(0, KE, KP)] if load in chunks else [(0, 3), (3, KC)]
    split_count = lambda load, part: sum(len(k_parts(l)) for l in loads[:loads.index(load)]) + part + 1
    all_split = lambda load: split_count(load, len(k_parts(load)) - 1)
    ctx_parts = [(0, i * KP, (i + 1) * KP) for i in range(PARTS)] + [(1, 0, KE)]

    with ExitStack() as ctx:
        sb = lambda name, shape, dt=F32: ctx.enter_context(nc.sbuf_tensor(name, shape, dt))
        ps = lambda name, shape: ctx.enter_context(nc.psum_tensor(name, shape, F32))
        sem = lambda name: ctx.enter_context(nc.semaphore(name))

        chl = sb("chl", [P, 2, KE, TOK], F32R)
        cip = sb("cip", [P, 2, KE, NIP], F32R)
        cipsq = sb("cipsq", [P, KE, NIP])
        raw = [sb(f"raw{i}", [P, KC * C]) for i in range(2)]
        whl = [sb(f"whl{i}", [P, 2, KE, KM * P], F32R) for i in range(2)]
        kst = [sb(f"kst{i}", [P, 2, HALF], F32R) for i in range(K_RING)]
        vst = [[sb(f"vst{e}{i}", [P, VC]) for i in range(2)] for e in range(2)]
        kip = sb("kip", [NIP, C])
        kipT = sb("kipT", [P, 2, G, NIP], F32R)
        gst = sb("gst", [L, B, L])
        ripn = sb("ripn", [P, NIP])
        nhalf = sb("nhalf", [P, NIP])
        ones = sb("ones", [P, P])
        ident = sb("ident", [NIP, NIP])

        ups = [ps(f"ups{i}", [P, 512]) for i in range(BANKS)]
        mps = [ps(f"mps{i}", [P, 512]) for i in range(2)]

        ctx_in = [sem(f"ctx_in{i}") for i in range(len(ctx_parts))]
        first_in = [sem(f"first_in{i}") for i in range(PARTS)]
        raw_in = [sem(f"raw_in{i}") for i in range(2)]
        c_hi, c_lo = sem("c_hi"), sem("c_lo")
        w_hi, w_lo = sem("w_hi"), sem("w_lo")
        consts, zeroed = sem("consts"), sem("zeroed")
        sq_done = sem("sq_done")
        u_ps = sem("u_ps")
        k_hi, k_lo = sem("k_hi"), sem("k_lo")
        k_out = [sem(f"k_out{i}") for i in range(K_RING)]
        v_cp = [sem(f"v_cp{e}") for e in range(2)]
        v_out = [[sem(f"v_out{e}{i}") for i in range(2)] for e in range(2)]
        kip_cp = [sem(f"kip_cp{e}") for e in range(2)]
        kipT_ps, kipT_hi, kipT_lo = sem("kipT_ps"), sem("kipT_hi"), sem("kipT_lo")
        norm_ps, norm_mx, norm_r = sem("norm_ps"), sem("norm_mx"), sem("norm_r")
        g_ps, g_cp, g_sc, g_out = sem("g_ps"), sem("g_cp"), sem("g_sc"), sem("g_out")
        w1_out = [sem(f"w1_out{i}") for i in range(2)]

        def units_of(chunk):
            j, c0, n = chunk
            if j in (K0, K1):
                return [(j, m, h) for h in range(2) for m in range(c0 // P, (c0 + n) // P)]
            return [(j, t, c0) for t in range(1 if j in (KIP, VIP) else TB)]

        units = [u for chunk in chunks for u in units_of(chunk)]
        index = {u: i for i, u in enumerate(units)}
        kunits = [u for u in units if u[0] in (K0, K1)]
        vunits = [u for u in units if u[0] in (V0, V1, VIP)]
        kindex = {u: i for i, u in enumerate(kunits)}
        vindex = {u: i for i, u in enumerate(vunits)}
        jobs_end = {chunk: index[units_of(chunk)[-1]] + 1 for chunk in chunks}
        rows_of = lambda j, t: NIP if j in (KIP, VIP) else min(P, TOK - t * P)
        kip_engine = lambda u: 0 if u[2] == 0 else 1

        def read_out(u):
            if u in kindex:
                return k_lo, kindex[u] + 1
            if u[0] == KIP:
                return kip_cp[kip_engine(u)], 1
            return v_cp[vindex[u] % 2], vindex[u] // 2 + 1

        def raw_view(load, q):
            if load in chunks:
                return raw[q % 2][:, 0:KE * load[2]].rearrange("p (k c) -> p k c", k=KE)
            n = S if load == X0 else C
            return raw[q % 2][:, 0:KC * n].rearrange("p (k c) -> p k c", k=KC)

        def split_target(load):
            if load in chunks:
                return whl[chunks.index(load) % 2][:, :, :, 0:load[2]]
            return {WQ1: wq_hl, WO1: wo_hl, X0: x_hl, WQ0: wq_hl, WO0: wo_hl}[load][:]

        block = ctx.enter_context(nc.Block())

        def load(queue, q, what, k0=0, k1=None):
            if what in chunks:
                j, c0, n = what
                src = weights[j][:, c0:c0 + n]
            else:
                src = x0 if what == X0 else later_weights[what]
            src = src.rearrange("(k p) c -> p k c", p=P)
            return queue.dma_start(raw_view(what, q)[:, k0:k1], src[:, k0:k1])

        def load_ctx(queue, i):
            h, k0, k1 = ctx_parts[i]
            at = slice(h * HALF, (h + 1) * HALF)
            queue.dma_start(craw[:, k0:k1, at], ctxT.rearrange("(k p) t -> p k t", p=P)[:, k0:k1, at]).then_inc(ctx_in[i], 16)

        @block.gpsimd
        def _(pool):
            nc.gpsimd.memset(ones[:], 1.0).then_inc(consts, 1)
            nc.gpsimd.memset(nhalf[:], -0.5).then_inc(consts, 1)
            nc.gpsimd.memset(ident[:], 0.0).then_inc(zeroed, 1)
            pool.wait_ge(zeroed, 1)
            nc.gpsimd.affine_select(out=ident[:], in_=ident[:], compare_op=ALU.not_equal, fill=1.0, base=0,
                                    pattern=[[-1, NIP]], channel_multiplier=1).then_inc(consts, 1)
            pool.wait_ge(ctx_in[PARTS - 1], 16)
            for q in range(1, len(loads)):
                if q >= 2:
                    pool.wait_ge(w_hi, all_split(loads[q - 2]))
                    pool.wait_ge(w_lo, all_split(loads[q - 2]))
                load(pool, q, loads[q]).then_inc(raw_in[q % 2], 16)
                if loads[q] == v0b:
                    pool.wait_ge(norm_mx, 1)
                    nc.gpsimd.tensor_tensor(ripn[:], ripn[:], nhalf[:], ALU.pow).then_inc(norm_r, 1)

        @block.sync
        def _(sp):
            def store_k(u):
                i = kindex[u]
                j, m, h = u
                sp.wait_ge(k_lo, i + 1)
                sp.wait_ge(k_hi, i + 1)
                for hl in range(2):
                    sp.dma_start(keys[0 if j == K0 else 1][h * NB_H:(h + 1) * NB_H, :, hl, m, :].rearrange("b p l -> p b l"),
                                 kst[i % K_RING][:, hl, :].bitcast(F32).rearrange("p (b l) -> p b l", l=L)).then_inc(k_out[i % K_RING], 16)

            def store_v(u):
                e, i = vindex[u] % 2, vindex[u] // 2
                j, t, c0 = u
                n = rows_of(j, t)
                sp.wait_ge(v_cp[e], i + 1)
                dst = values_ip if j == VIP else values[0 if j == V0 else 1][t * P:t * P + n, :]
                sp.dma_start(dst[:, c0:c0 + VC], vst[e][i % 2][0:n, :]).then_inc(v_out[e][i % 2], 16)

            for i in range(PARTS):
                load(sp, 0, loads[0], *k_parts(loads[0])[i]).then_inc(first_in[i], 16)
                load_ctx(sp, i)
            load_ctx(sp, PARTS)
            for chunk in chunks:
                for u in units_of(chunk):
                    if u in kindex:
                        store_k(u)
                    elif u in vindex:
                        store_v(u)
                if chunk == kipb:
                    sp.wait_ge(g_cp, B)
                    sp.wait_ge(g_sc, B)
                    sp.dma_start(gram.rearrange("b r l -> r b l"), gst[:]).then_inc(g_out, 16)
                for i, what in enumerate((WQ1, WO1)):
                    if what in beside.get(chunk, []):
                        sp.wait_ge(w_hi, all_split(what))
                        sp.wait_ge(w_lo, all_split(what))
                        sp.dma_start(split_weights[i], (wq_hl, wo_hl)[i][:].bitcast(F32)).then_inc(w1_out[i], 16)
            for r in range(K_RING):
                sp.wait_ge(k_out[r], 32 * len(range(r, len(kunits), K_RING)))
            for e in range(2):
                for r in range(2):
                    sp.wait_ge(v_out[e][r], 16 * len(range(2 * r + e, len(vunits), 4)))
            sp.wait_ge(g_out, 16)
            for i in range(2):
                sp.wait_ge(w1_out[i], 16)

        @block.scalar
        def _(act):
            def split_ctx(i):
                h, k0, k1 = ctx_parts[i]
                at = slice(h * HALF, (h + 1) * HALF)
                act.wait_ge(ctx_in[i], 16)
                nc.scalar.activation(chl[:, 0, k0:k1, at], craw[:, k0:k1, at], ACT.Copy).then_inc(c_hi, 1)

            def split(q, part):
                what = loads[q]
                if q == 0:
                    act.wait_ge(first_in[part], 16)
                elif part == 0:
                    act.wait_ge(raw_in[q % 2], 16 * (q // 2 + q % 2))
                if part == 0 and what in chunks and chunks.index(what) >= 2:
                    act.wait_ge(u_ps, jobs_end[chunks[chunks.index(what) - 2]])
                if part == 0 and what == X0:
                    act.wait_ge(g_ps, B)
                    act.wait_ge(c_lo, len(ctx_parts))
                    act.wait_ge(sq_done, 3)
                if part == 0 and what in (WQ0, WO0):
                    act.wait_ge(w1_out[(WQ0, WO0).index(what)], 16)
                k0, k1 = k_parts(what)[part]
                nc.scalar.activation(split_target(what)[:, 0, k0:k1], raw_view(what, q)[:, k0:k1], ACT.Copy).then_inc(w_hi, 1)

            def evac(u):
                act.wait_ge(u_ps, index[u] + 1)
                bank = ups[index[u] % BANKS]
                j = u[0]
                if u in kindex:
                    i = kindex[u]
                    if i >= K_RING:
                        act.wait_ge(k_out[i % K_RING], 32 * (i // K_RING))
                    n = L if j == K0 else L_TEXT
                    nc.scalar.activation(kst[i % K_RING][:, 0, :].rearrange("p (b l) -> p b l", l=L)[:, :, 0:n],
                                         bank[:, 0:HALF].rearrange("p (b l) -> p b l", l=L)[:, :, 0:n],
                                         ACT.Copy).then_inc(k_hi, 1)
                elif j == KIP:
                    nc.scalar.activation(kip[:, u[2]:u[2] + VC], bank[0:NIP, 0:VC], ACT.Copy).then_inc(kip_cp[0], 1)
                else:
                    i, n = vindex[u] // 2, rows_of(j, u[1])
                    if i >= 2:
                        act.wait_ge(v_out[0][i % 2], 16 * (i // 2))
                    nc.scalar.activation(vst[0][i % 2][0:n, :], bank[0:n, 0:VC], ACT.Copy).then_inc(v_cp[0], 1)

            for i in range(PARTS):
                split(0, i)
                split_ctx(i)
            split_ctx(PARTS)
            def split_both(what):
                for part in range(len(k_parts(what))):
                    split(loads.index(what), part)

            for i, chunk in enumerate(chunks):
                for what in chunks[i + 1:i + 2]:
                    split_both(what)
                for n, u in enumerate(units_of(chunk)):
                    if n == 3:
                        for what in beside.get(chunk, []):
                            split_both(what)
                    if u in kindex or u[0] == KIP and kip_engine(u) == 0 or u in vindex and vindex[u] % 2 == 0:
                        evac(u)
                if chunk == v0b:
                    for b in range(B):
                        act.wait_ge(g_ps, b + 1)
                        nc.scalar.activation(gst[:, b, 0:L_TEXT], mps[b % 2][0:L, 0:L_TEXT], ACT.Copy).then_inc(g_cp, 1)
                if chunk == kipb:
                    act.wait_ge(kipT_ps, 1)
                    nc.scalar.activation(kipT[:, 0], mps[1][:, 0:G * NIP].rearrange("p (g t) -> p g t", t=NIP),
                                         ACT.Copy).then_inc(kipT_hi, 1)

        @block.vector
        def _(dve):
            def split_ctx(i):
                h, k0, k1 = ctx_parts[i]
                at = slice(h * HALF, (h + 1) * HALF)
                dve.wait_ge(c_hi, i + 1)
                nc.vector.tensor_tensor(chl[:, 1, k0:k1, at], craw[:, k0:k1, at], chl[:, 0, k0:k1, at].bitcast(F32),
                                        ALU.subtract).then_inc(c_lo, 1)

            def split(q, part):
                what = loads[q]
                dve.wait_ge(w_hi, split_count(what, part))
                k0, k1 = k_parts(what)[part]
                w = split_target(what)
                nc.vector.tensor_tensor(w[:, 1, k0:k1], raw_view(what, q)[:, k0:k1], w[:, 0, k0:k1].bitcast(F32),
                                        ALU.subtract).then_inc(w_lo, 1)

            def evac(u):
                bank = ups[index[u] % BANKS]
                j = u[0]
                if u in kindex:
                    i = kindex[u]
                    _, m, h = u
                    n = L if j == K0 else L_TEXT
                    dve.wait_ge(k_hi, i + 1)
                    view = lambda a: a.rearrange("p (b l) -> p b l", l=L)
                    kv = [view(kst[i % K_RING][:, hl, :]) for hl in range(2)]
                    if j == K1:
                        dve.wait_ge(kipT_lo, 1)
                        for hl in range(2):
                            nc.vector.tensor_copy(
                                kv[hl][:, :, L_TEXT:L],
                                kipT[:, hl, m, h * NB_H * N_IP:(h + 1) * NB_H * N_IP].bitcast(F32).rearrange("p (b n) -> p b n", n=N_IP))
                    nc.vector.tensor_tensor(kv[1][:, :, 0:n], view(bank[:, 0:HALF])[:, :, 0:n],
                                            kv[0][:, :, 0:n].bitcast(F32), ALU.subtract).then_inc(k_lo, 1)
                    return
                dve.wait_ge(u_ps, index[u] + 1)
                if j == KIP:
                    nc.vector.tensor_copy(kip[:, u[2]:u[2] + VC], bank[0:NIP, 0:VC]).then_inc(kip_cp[1], 1)
                else:
                    i, n = vindex[u] // 2, rows_of(j, u[1])
                    if i >= 2:
                        dve.wait_ge(v_out[1][i % 2], 16 * (i // 2))
                    nc.vector.tensor_copy(vst[1][i % 2][0:n, :], bank[0:n, 0:VC]).then_inc(v_cp[1], 1)

            for i in range(PARTS):
                split(0, i)
                split_ctx(i)
            split_ctx(PARTS)
            def split_both(what):
                for part in range(len(k_parts(what))):
                    split(loads.index(what), part)

            for i, chunk in enumerate(chunks):
                for what in chunks[i + 1:i + 2]:
                    split_both(what)
                if chunk == k0b:
                    dve.wait_ge(c_lo, len(ctx_parts))
                    for hl in range(2):
                        src = chl[:, hl].bitcast(F32).rearrange("p k (b l) -> p k b l", l=L)[:, :, :, L_TEXT:L]
                        nc.vector.tensor_copy(cip[:, hl].rearrange("p k (b n) -> p k b n", n=N_IP), src).then_inc(sq_done, 1)
                    src = craw[:].rearrange("p k (b l) -> p k b l", l=L)[:, :, :, L_TEXT:L]
                    nc.vector.tensor_tensor(cipsq[:].rearrange("p k (b n) -> p k b n", n=N_IP), src, src,
                                            ALU.mult).then_inc(sq_done, 1)
                for n, u in enumerate(units_of(chunk)):
                    if n == 3:
                        for what in beside.get(chunk, []):
                            split_both(what)
                    if u in kindex or u[0] == KIP and kip_engine(u) == 1 or u in vindex and vindex[u] % 2 == 1:
                        evac(u)
                if chunk == k0b:
                    dve.wait_ge(norm_ps, 1)
                    nc.vector.tensor_scalar(ripn[:], mps[0][:, 0:NIP], EPS * EPS, None, ALU.max).then_inc(norm_mx, 1)
                if chunk == v0b:
                    dve.wait_ge(norm_r, 1)
                    for b in range(B):
                        dve.wait_ge(g_cp, b + 1)
                        nc.vector.scalar_tensor_tensor(
                            out=gst[:, b, L_TEXT:L], in0=mps[b % 2][0:L, L_TEXT:L], scalar=SEM_SCALE,
                            in1=ripn[0:L, b * N_IP:(b + 1) * N_IP], op0=ALU.mult, op1=ALU.mult).then_inc(g_sc, 1)
                if chunk == kipb:
                    dve.wait_ge(kipT_hi, 1)
                    nc.vector.tensor_tensor(kipT[:, 1], mps[1][:, 0:G * NIP].rearrange("p (g t) -> p g t", t=NIP),
                                            kipT[:, 0].bitcast(F32), ALU.subtract).then_inc(kipT_lo, 1)

        @block.tensor
        def _(pe):
            for chunk in chunks:
                j, c0, n_cols = chunk
                w = whl[chunks.index(chunk) % 2]
                for u in units_of(chunk):
                    i = index[u]
                    bank = ups[i % BANKS]
                    new_chunk = u == units_of(chunk)[0]
                    if i >= BANKS:
                        pe.wait_ge(*read_out(units[i - BANKS]))
                    if chunk == chunks[0] and u[2] == 1 or j == KIP:
                        pe.wait_ge(c_lo, len(ctx_parts))
                    if j == KIP:
                        pe.wait_ge(sq_done, 2)
                    for k in range(KE):
                        if new_chunk and k % KP == 0:
                            if chunk == chunks[0]:
                                pe.wait_ge(c_lo, k // KP + 1)
                            pe.wait_ge(w_lo, split_count(chunk, k // KP))
                        for a, b in PASSES:
                            flags = dict(start=(k == 0 and a == b == 0), stop=(k == KE - 1 and a == 1))
                            if u in kindex:
                                _, m, h = u
                                mm = nc.tensor.matmul(bank[:, 0:HALF], w[:, a, k, m * P - c0:(m + 1) * P - c0],
                                                      chl[:, b, k, h * HALF:(h + 1) * HALF], **flags)
                            else:
                                source, n = cip if j in (KIP, VIP) else chl, rows_of(j, u[1])
                                mm = nc.tensor.matmul(bank[0:n, 0:VC], source[:, b, k, u[1] * P:u[1] * P + n],
                                                      w[:, a, k, 0:VC], **flags)
                    mm.then_inc(u_ps, 1)
                if chunk == k0b:
                    pe.wait_ge(sq_done, 3)
                    pe.wait_ge(consts, 3)
                    for k in range(KE):
                        mm = nc.tensor.matmul(mps[0][:, 0:NIP], ones[:], cipsq[:, k, :], start=(k == 0), stop=(k == KE - 1))
                    mm.then_inc(norm_ps, 1)
                if chunk == v0b:
                    for b in range(B):
                        if b == 0:
                            pe.wait_ge(norm_mx, 1)
                        if b >= 2:
                            pe.wait_ge(g_sc, b - 1)
                        for k in range(KE):
                            t = craw[:, k, b * L:(b + 1) * L]
                            mm = nc.tensor.matmul(mps[b % 2][0:L, 0:L], t, t, start=(k == 0), stop=(k == KE - 1))
                        mm.then_inc(g_ps, 1)
                if chunk == kipb:
                    for e in range(2):
                        pe.wait_ge(kip_cp[e], 1)
                    pe.wait_ge(g_sc, B)
                    for m in range(G):
                        mm = nc.tensor.transpose(mps[1][:, m * NIP:(m + 1) * NIP], kip[:, m * P:(m + 1) * P], ident[:])
                    mm.then_inc(kipT_ps, 1)


def attention_block(nc, xs, split_weights, bias, keys, values, mask, values_ip, gram, wq_hl, wo_hl, x_hl):
    PV_LAG = (6, 7)
    NEWTON = 4 * NEWTON_STEPS
    keys_of = lambda layer: (L, L_TEXT)[layer]
    row_parts = lambda n: [slice(0, n)] if n == L else [slice(0, n - 1), slice(n - 1, n)]
    TEXT_DMAS = len(row_parts(L_TEXT))

    with ExitStack() as ctx:
        sb = lambda name, shape, dt=F32: ctx.enter_context(nc.sbuf_tensor(f"a_{name}", shape, dt))
        ps = lambda name, shape: ctx.enter_context(nc.psum_tensor(f"a_{name}", shape, F32))
        sem = lambda name: ctx.enter_context(nc.semaphore(f"a_{name}"))

        q_hl = sb("q_hl", [P, 2, G, S], F32R)
        o_hl = [sb(f"o_hl{i}", [P, 2, G, S], F32R) for i in range(2)]
        key_bd = sb("key_bd", [P, 2, G, GL], F32R)
        val = sb("val", [P, C])
        xraw = [sb(f"xraw{i}", [P, S]) for i in range(2)]
        res = [sb(f"res{i}", [P, S]) for i in range(2)]
        outs = [sb(f"outs{i}", [P, S]) for i in range(2)]
        ident = sb("ident", [P, P])
        bias_c = sb("bias_c", [P, 2, KC])
        mask_c = sb("mask_c", [P, NT])
        row_max = sb("row_max", [P, 2 * HG])
        den = sb("den", [P, 2, 2 * HG])
        gm = sb("gm", [P, WIN])
        prod = [sb(f"prod{i}", [P, NT, L]) for i in range(2)]
        norm2 = [sb(f"norm2{i}", [P, HG, NT]) for i in range(2)]
        y = [sb(f"y{i}", [P, HG, NT]) for i in range(2)]
        yx = [sb(f"yx{i}", [P, HG, NT]) for i in range(2)]
        three_halves = sb("three_halves", [P, HG, NT])
        att = sb("att", [P, G, NT, HG, N_IP])
        dot = [sb(f"dot{i}", [P, HG, NT, N_IP]) for i in range(2)]
        fused = sb("fused", [P, NT, HG, N_IP])
        ip_max = sb("ip_max", [P, NT, HG])
        ip_den = sb("ip_den", [P, NT, HG])
        pip = sb("pip", [P, NT, WIN_IP])
        e = sb("e", [P, G, E_ROW])
        pT = [sb(f"pT{i}", [P, HG, S]) for i in range(2)]

        proj_ps = [ps(f"proj_ps{i}", [P, S]) for i in range(2)]
        s_ps = ps("s_ps", [P, 2, 512])
        t_ps = ps("t_ps", [P, 2, S])
        o_ps = ps("o_ps", [P, S])
        g_ps = ps("g_ps", [P, NT, WIN])

        w1_in = [sem(f"w1_in{c}") for c in range(KC)]
        small_in = sem("small_in")
        zeroed, keys_zeroed, ident_0 = sem("zeroed"), sem("keys_zeroed"), sem("ident_0")
        consts, ones_set = sem("consts"), sem("ones_set")
        x_in = [sem(f"x_in{i}") for i in range(2)]
        res_in = [sem(f"res_in{i}") for i in range(2)]
        out_done = [sem(f"out_done{i}") for i in range(2)]
        tail_in = sem("tail_in")
        key_in = [sem(f"key_in{i}") for i in range(G)]
        val_in = sem("val_in")
        x_hi, x_lo = sem("x_hi"), sem("x_lo")
        qp_ready, op_ready = sem("qp_ready"), sem("op_ready")
        q_hi, q_lo = sem("q_hi"), sem("q_lo")
        s_ready, max_done, sub_done, exp_done = sem("s_ready"), sem("max_done"), sem("sub_done"), sem("exp_done")
        den_done, rden_done, prob_done = sem("den_done"), sem("rden_done"), sem("prob_done")
        t_ready, t_copied = sem("t_ready"), sem("t_copied")
        pv_ready, o_hi, o_lo = sem("pv_ready"), sem("o_hi"), sem("o_lo")
        y_out = sem("y_out")
        att_done = sem("att_done")
        valip_in, gm_in = sem("valip_in"), sem("gm_in")
        g_ready, prod_done, dot_done, norm_done = sem("g_ready"), sem("prod_done"), sem("dot_done"), sem("norm_done")
        seed_step, newton, dotn_done = sem("seed_step"), sem("newton"), sem("dotn_done")
        ip_step, ip_exp, pip_done = sem("ip_step"), sem("ip_exp"), sem("pip_done")
        it_ready, it_copied = sem("it_ready"), sem("it_copied")

        e_v = [e[:, g, 0:NT * GL].rearrange("p (t h l) -> p t h l", t=NT, h=HG) for g in range(G)]
        xs = [x.rearrange("b (k p) s -> b k p s", p=P) for x in xs]

        def schedule(engine, half):
            half(0, 0, 0, None, 0)
            half(1, 1, 0, 0, 0)
            with engine.Fori(0, (B - 4) // 2) as pair:
                half(2 * pair + 2, 0, 0, 0, 0)
                half(2 * pair + 3, 1, 0, 0, 0)
            half(B - 2, 0, 0, 0, 0)
            half(B - 1, 1, 0, 0, 1)
            half(B, 0, 1, 0, 1)
            with engine.Fori(0, (B - 2) // 2) as pair:
                half(2 * pair + B + 1, 1, 1, 1, 1)
                half(2 * pair + B + 2, 0, 1, 1, 1)
            half(2 * B - 1, 1, 1, 1, None)
            half(2 * B, 0, None, 1, None)

        def of(n, parity, cur, prev, slot, lag, count, stride=1, layers=(0, 1)):
            for back in range(2):
                i, rest = divmod(slot + SLOTS * back - lag, stride)
                layer = prev if back else cur
                if rest == 0 and 0 <= i < count and layer in layers:
                    return n - back, parity ^ back, i, layer
            return None

        def s_unit(*a):
            return of(*a, lag=1, count=2 * G)

        def t_unit(*a):
            return of(*a, lag=4, count=2 * G)

        def pv_unit(*a):
            return of(*a, lag=PV_LAG[0], count=G, stride=2, layers=(0,)) or ip_pv_unit(*a)

        def ip_pv_unit(*a):
            return of(*a, lag=PV_LAG[1], count=G, stride=2, layers=(1,))

        def norm_unit(*a):
            return of(*a, lag=6, count=G, stride=2, layers=(1,))

        def first(m, i=0):
            return isinstance(m, int) and m == 0 and i == 0

        def ring_count(m, par, k):
            return 8 * KC * (m - par) + 16 * ((par * KC + k) // 2 + 1)

        def x_count(m, par, k):
            return ring_count(m, par, k) - 16 * ((KC + 1 - (par * KC + k) % 2) // 2)

        def load_x(sp, m, k, layer, par):
            i = (m - 1) * KC + k
            ring = (par * KC + k) % 2
            if layer == 1:
                sp.wait_ge(out_done[ring], ring_count(m - B, par, k) if isinstance(m, int) else 8 * B * G)
            if not (isinstance(m, int) and i < 2):
                sp.wait_ge(x_hi, i - 1)
                sp.wait_ge(x_lo, i - 1)
            sp.dma_start(xraw[ring][:], xs[layer][m - B * layer, k]).then_inc(x_in[ring], 16)

        def load_res(sp, m, par, c, layer):
            ring = (par * G + c) % 2
            if c >= 2:
                sp.wait_ge(y_out, m * G + c - 1)
            sp.dma_start(res[ring][:], xs[layer][m - B * layer, c]).then_inc(res_in[ring], 16)

        def store_out(sp, m, par, c, layer, source=None):
            sp.wait_ge(y_out, m * G + c + 1)
            ring = (par * G + c) % 2
            sp.dma_start(xs[layer + 1][m - B * layer, c], outs[ring][:] if source is None else source).then_inc(out_done[ring], 16)

        tail_banks = [proj_ps[1][:], proj_ps[0][:], s_ps[:, 0], s_ps[:, 1], t_ps[:, 0]]
        tail_res = [x_hl[:, 0, c, :].bitcast(F32) for c in range(KC)]
        tail_outs = [e[:, c, 0:S] for c in range(KC)]
        TAIL = {0: [(0, [0, 1])], 1: [(1, [0, 1])], 2: [(0, [2]), (2, [0, 1, 2])], 3: [(1, [2]), (3, [0, 1, 2])],
                4: [(0, [3]), (1, [3]), (4, [0, 1, 2, 3])], 5: [(2, [3]), (3, [3])]}

        def load_w1(sp, i, c):
            sp.wait_ge((qp_ready, op_ready)[i], G * (B - 1) + c + 1)
            cols = slice(c * P, (c + 1) * P)
            sp.dma_start((wq_hl, wo_hl)[i][:, :, :, cols].bitcast(F32), split_weights[i][:, :, :, cols]).then_inc(w1_in[c], 16)

        def load_keys(sp, m, g, layer):
            for j in range(HG):
                rows = slice(j * D, (j + 1) * D)
                sp.dma_start(key_bd[rows, :, g, j * L:(j + 1) * L].bitcast(F32),
                             keys[layer][m - B * layer, rows, :, g, :]).then_inc(key_in[g], 16)

        def load_gram(sp, r):
            for rows in row_parts(L_TEXT):
                sp.dma_start(gm[rows, 0:L], gram[r, rows]).then_inc(gm_in, 16)

        def load_values(sp, m, layer):
            b = m - B * layer
            if isinstance(m, int) and m == B:
                sp.dma_start(val[L_TEXT:L, :], val[WIN - N_IP:WIN, :]).then_inc(val_in, 16)
            for rows in row_parts(keys_of(layer)):
                sp.dma_start(val[rows, :], values[layer].rearrange("(b l) c -> b l c", l=L)[b, rows]).then_inc(val_in, 16)
            if layer == 1:
                vip = values_ip.rearrange("(b n) (g j d) -> b n g j d", n=N_IP, j=HG, d=D)
                for j in range(HG):
                    rows = slice(WIN + j * N_IP, WIN + (j + 1) * N_IP)
                    sp.dma_start(val[rows, :].rearrange("p (g j d) -> p g j d", j=HG, d=D)[:, :, j, :],
                                 vip[b, :, :, j, :]).then_inc(valip_in, 16)

        def values_count(m, layer):
            return 16 * (m + 1) if layer == 0 else 16 * (B + 1) + 16 * TEXT_DMAS * (m - B + 1)

        def pair_view(u):
            m, par, i, layer = u
            g, tp = divmod(i, 2)
            return e_v[g][:, 2 * tp:2 * tp + 2, :, 0:keys_of(layer)]

        def split_x_lo(pool, n, k, par):
            i = (n - 1) * KC + k
            pool.wait_ge(x_hi, i + 1)
            nc.gpsimd.tensor_tensor(x_hl[:, 1, k, :], xraw[(par * KC + k) % 2][:], x_hl[:, 0, k, :].bitcast(F32),
                                    ALU.subtract).then_inc(x_lo, 1)

        def normalise(pool, m, par, i, layer):
            pool.wait_ge(rden_done, 10 * m + i + 1)
            r = den[:, 1, :].rearrange("p (t h) -> p t h", h=HG)
            v = pair_view((m, par, i, layer))
            nc.gpsimd.tensor_tensor(v, v, r.unsqueeze(3).to_broadcast([P, 2, HG, keys_of(layer)]), ALU.mult).then_inc(prob_done, 1)

        def refine_norm(pool, m, par, g, layer):
            two = (par * G + g) % 2
            i = G * (m - B) + g
            base = NEWTON * i
            pool.wait_ge(seed_step, 3 * i + 3)
            for step in range(NEWTON_STEPS):
                c = base + 4 * step
                if step:
                    pool.wait_ge(newton, c)
                nc.gpsimd.tensor_tensor(yx[two][:], y[two][:], y[two][:], ALU.mult).then_inc(newton, 1)
                pool.wait_ge(newton, c + 1)
                nc.gpsimd.tensor_tensor(yx[two][:], yx[two][:], norm2[two][:], ALU.mult).then_inc(newton, 1)
                pool.wait_ge(newton, c + 2)
                nc.gpsimd.tensor_tensor(yx[two][:], three_halves[:], yx[two][:], ALU.subtract).then_inc(newton, 1)
                pool.wait_ge(newton, c + 3)
                nc.gpsimd.tensor_tensor(y[two][:], y[two][:], yx[two][:], ALU.mult).then_inc(newton, 1)
            pool.wait_ge(newton, base + NEWTON)
            pool.wait_ge(dot_done, HG * i + HG)
            for h in range(HG):
                last = nc.gpsimd.tensor_tensor(dot[two][:, h], dot[two][:, h], y[two][:, h].unsqueeze(2).to_broadcast([P, NT, N_IP]),
                                               ALU.mult)
            last.then_inc(dotn_done, 1)

        block = ctx.enter_context(nc.Block())

        @block.sync
        def _(sp):
            for g in range(G):
                sp.wait_ge(keys_zeroed, g + 1)
                load_keys(sp, 0, g, 0)
            sp.wait_ge(zeroed, 2)
            load_values(sp, 0, 0)
            load_gram(sp, 0)
            for layer in range(2):
                sp.dma_start(bias_c[:, layer], bias[layer]).then_inc(small_in, 16)
            sp.dma_start(mask_c[:], mask).then_inc(small_in, 16)

            def half(n, par, cur, prev, nxt):
                has_cur, has_prev, more = cur is not None, prev is not None, nxt is not None
                if not has_cur:
                    sp.wait_ge(qp_ready, G * n)
                    for c in range(KC):
                        sp.dma_start(tail_res[c], xs[prev][n - 1 - B * prev, c]).then_inc(tail_in, 16)
                    for c in range(KC):
                        store_out(sp, n - 1, 1 - par, c, prev, tail_outs[c])
                    return
                for slot in range(SLOTS):
                    if slot == 4 and prev == 1 and cur == 1:
                        sp.wait_ge(g_ready, 20 * (n - B))
                        load_gram(sp, n - B)
                    if slot in (3, 4) and has_prev:
                        load_res(sp, n - 1, 1 - par, slot - 3, prev)
                    if slot in (3, 4) and more:
                        load_x(sp, n + 1, slot - 3, nxt, 1 - par)
                    if slot == 1 and has_prev and has_cur:
                        sp.wait_ge(s_ready, 10 * n)
                        load_keys(sp, n, G - 1, cur)
                    if has_cur and more and slot in (3, 5, 7, 9):
                        g = (slot - 3) // 2
                        sp.wait_ge(s_ready, 10 * n + 2 * g + 2)
                        load_keys(sp, n + 1, g, nxt)
                    if slot == 5 and has_prev and has_cur:
                        sp.wait_ge(pv_ready, G * n)
                        load_values(sp, n, cur)
                    if slot >= 5 and more and slot < 8:
                        load_x(sp, n + 1, slot - 3, nxt, 1 - par)
                    if isinstance(n, int) and n == B - 1 and 3 <= slot < 3 + KC:
                        load_w1(sp, 0, slot - 3)
                    if isinstance(n, int) and n == B and slot > G:
                        load_w1(sp, 1, slot - G - 1)
                    if slot >= 6 and has_prev:
                        store_out(sp, n - 1, 1 - par, slot - 6, prev)
                    if slot >= 5 and slot < 8 and has_prev:
                        load_res(sp, n - 1, 1 - par, slot - 3, prev)
                if isinstance(n, int) and n == B:
                    load_w1(sp, 1, KC - 1)
                if has_prev:
                    store_out(sp, n - 1, 1 - par, G - 1, prev)

            schedule(sp, half)
            for r in range(2):
                sp.wait_ge(out_done[r], 16 * (2 * B * G // 2))

        @block.gpsimd
        def _(pool):
            for zeros in (val, gm):
                nc.gpsimd.memset(zeros[:], 0.0).then_inc(zeroed, 1)
            nc.gpsimd.memset(three_halves[:], 1.5).then_inc(consts, 1)
            nc.gpsimd.memset(pip[:, :, 0:WIN], 0.0).then_inc(consts, 1)
            nc.gpsimd.memset(ident[:], 0.0).then_inc(ident_0, 1)
            pool.wait_ge(ident_0, 1)
            nc.gpsimd.affine_select(out=ident[:], in_=ident[:], compare_op=ALU.not_equal, fill=1.0, base=0,
                                    pattern=[[-1, P]], channel_multiplier=1).then_inc(consts, 1)
            nc.gpsimd.memset(e[:, :, NT * GL:E_ROW], 0.0).then_inc(consts, 1)

            def half(n, par, cur, prev, nxt):
                for slot in range(SLOTS):
                    a = (n, par, cur, prev, slot)
                    if u := norm_unit(*a):
                        refine_norm(pool, *u)
                    if u := s_unit(*a):
                        normalise(pool, *u)
                    if (u := of(*a, lag=6, count=G, stride=2, layers=(0,))) and isinstance(u[0], int) and u[0] == B - 1:
                        pool.wait_ge(t_ready, 10 * u[0] + 2 * u[2] + 2)
                        nc.gpsimd.memset(e_v[u[2]][:, :, :, L_TEXT:L], 1.0).then_inc(ones_set, 1)
                    if slot >= 5 and nxt is not None:
                        split_x_lo(pool, n + 1, slot - 5, 1 - par)

            schedule(pool, half)

        @block.scalar
        def _(act):
            def split_x_hi(n, k, par):
                ring = (par * KC + k) % 2
                act.wait_ge(x_in[ring], x_count(n, par, k))
                if k == 0:
                    act.wait_ge(qp_ready, G * n)
                nc.scalar.activation(x_hl[:, 0, k, :], xraw[ring][:], ACT.Copy).then_inc(x_hi, 1)

            def half(n, par, cur, prev, nxt):
                has_cur, has_prev, more = cur is not None, prev is not None, nxt is not None
                for slot in range(SLOTS):
                    a = (n, par, cur, prev, slot)
                    ipu = ip_pv_unit(*a)
                    if not ipu and (u := pv_unit(*a)):
                        evac_o(*u)
                    u = t_unit(*a)
                    if u:
                        m, mp, i, _ = u
                        g, hp = divmod(i, 2)
                        act.wait_ge(t_ready, 10 * m + i + 1)
                        buf = pT[(mp * G + g) % 2]
                        nc.scalar.activation(buf[0:WIN, 2 * hp:2 * hp + 2, :], t_ps[0:WIN], ACT.Copy).then_inc(t_copied, 1)
                    if v := of(*a, lag=5, count=2 * G, layers=(1,)):
                        copy_dot(*v, 1)
                    if ipu:
                        act.wait_ge(it_ready, G * (ipu[0] - B) + ipu[2] + 1)
                        nc.scalar.activation(pT[(ipu[1] * G + ipu[2]) % 2][WIN:WIN_IP],
                                             o_ps[WIN:WIN_IP, :].unsqueeze(1).to_broadcast([HG * N_IP, HG, S]),
                                             ACT.Copy).then_inc(it_copied, 1)
                    if v := s_unit(*a):
                        m, mp, i, layer = v
                        act.wait_ge(sub_done, 10 * m + i + 1)
                        if layer == 1:
                            g, tp = divmod(i, 2)
                            nc.scalar.activation(att[:, g, 2 * tp:2 * tp + 2],
                                                 s_ps[:, :, 0:GL].rearrange("p b (h l) -> p b h l", l=L)[:, :, :, L_TEXT:L],
                                                 ACT.Copy).then_inc(att_done, 1)
                        nc.scalar.activation(pair_view(v), pair_view(v), ACT.Exp, scale=SCALE).then_inc(exp_done, 1)
                    if ipu:
                        evac_o(*ipu)
                    if u and u[3] == 1:
                        copy_dot(*u, 0)
                    if slot < G and has_cur:
                        act.wait_ge(qp_ready, G * n + slot + 1)
                        nc.scalar.activation(q_hl[:, 0, slot, :], proj_ps[slot % 2][:], ACT.Copy).then_inc(q_hi, 1)
                    if slot >= G and more:
                        split_x_hi(n + 1, slot - G, 1 - par)
                    if v := norm_unit(*a):
                        m, _, g, _ = v
                        act.wait_ge(ip_step, 5 * (G * (m - B) + g) + 3)
                        nc.scalar.activation(fused[:], fused[:], ACT.Exp).then_inc(ip_exp, 1)

            def copy_dot(m, mp, i, layer, hh):
                g, hp = divmod(i, 2)
                r = m - B
                act.wait_ge(prod_done, 20 * r + 2 * i + hh + 1)
                if hp == 0 and hh == 0 and not (isinstance(r, int) and G * r + g < 2):
                    act.wait_ge(ip_step, 5 * (G * r + g - 2) + 1)
                nc.scalar.activation(dot[(mp * G + g) % 2][:, 2 * hp + hh], prod[hh][:, :, L_TEXT:L], ACT.Copy).then_inc(dot_done, 1)

            def evac_o(m, mp, g, layer):
                act.wait_ge(pv_ready, G * m + g + 1)
                nc.scalar.activation(o_hl[mp][:, 0, g, :], o_ps[:], ACT.Copy).then_inc(o_hi, 1)

            schedule(act, half)

        @block.vector
        def _(dve):
            for g in range(G):
                nc.vector.memset(key_bd[:, :, g].bitcast(F32), 0.0).then_inc(keys_zeroed, 1)

            def split_o_lo(m, mp, g, layer):
                dve.wait_ge(o_hi, G * m + g + 1)
                nc.vector.tensor_tensor(o_hl[mp][:, 1, g, :], o_ps[:], o_hl[mp][:, 0, g, :].bitcast(F32),
                                        ALU.subtract).then_inc(o_lo, 1)

            def softmax_front(m, mp, i, layer):
                g, tp = divmod(i, 2)
                LT = keys_of(layer)
                src = s_ps[:, :, 0:GL].rearrange("p b (h l) -> p b h l", l=L)[:, :, :, 0:LT]
                mx = row_max[:].rearrange("p (t h) -> p t h", h=HG)
                dve.wait_ge(s_ready, 10 * m + i + 1)
                nc.vector.tensor_reduce(mx, src, AX.X, ALU.max).then_inc(max_done, 1)
                dve.wait_ge(max_done, 10 * m + i + 1)
                nc.vector.tensor_tensor(pair_view((m, mp, i, layer)), src, mx.unsqueeze(3).to_broadcast([P, 2, HG, LT]),
                                        ALU.subtract).then_inc(sub_done, 1)

            def key_sums(m, mp, i, layer):
                c = 10 * m + i + 1
                dve.wait_ge(exp_done, c)
                nc.vector.tensor_reduce(den[:, 0, :].rearrange("p (t h) -> p t h", h=HG), pair_view((m, mp, i, layer)),
                                        AX.X, ALU.add).then_inc(den_done, 1)

            def key_sums_inverse(m, mp, i, layer):
                c = 10 * m + i + 1
                if not (isinstance(m, int) and c == 1):
                    dve.wait_ge(prob_done, c - 1)
                dve.wait_ge(den_done, c)
                nc.vector.reciprocal(den[:, 1, :], den[:, 0, :]).then_inc(rden_done, 1)

            def context_norm(m, mp, i, layer, hh):
                g, hp = divmod(i, 2)
                h = 2 * hp + hh
                r = m - B
                c = 20 * r + 2 * i + hh + 1
                dve.wait_ge(g_ready, c)
                if hp == 0 and hh == 0 and not (isinstance(r, int) and G * r + g < 2):
                    dve.wait_ge(newton, NEWTON * (G * r + g - 1))
                if not (isinstance(r, int) and c < 3):
                    dve.wait_ge(norm_done, c - 2)
                    dve.wait_ge(dot_done, c - 2)
                nc.vector.tensor_tensor(prod[hh][:], g_ps[:, :, 0:L], e_v[g][:, :, h, :], ALU.mult).then_inc(prod_done, 1)
                dve.wait_ge(prod_done, c)
                nc.vector.tensor_reduce(norm2[(mp * G + g) % 2][:, h, :], prod[hh][:, :, 0:L_TEXT], AX.X, ALU.add).then_inc(norm_done, 1)

            def norm_seed(m, mp, g, layer):
                two = (mp * G + g) % 2
                r = m - B
                c = 3 * (G * r + g)
                dve.wait_ge(norm_done, HG * (G * r + g) + HG)
                nc.vector.tensor_scalar(norm2[two][:], norm2[two][:], EPS * EPS, 0.5, ALU.max, ALU.mult).then_inc(seed_step, 1)
                if not (isinstance(r, int) and G * r + g < 2):
                    dve.wait_ge(dotn_done, G * r + g - 1)
                dve.wait_ge(seed_step, c + 1)
                nc.vector.tensor_scalar(y[two][:].bitcast(I32), norm2[two][:].bitcast(I32), 1, None,
                                        ALU.arith_shift_right).then_inc(seed_step, 1)
                dve.wait_ge(seed_step, c + 2)
                nc.vector.tensor_scalar(y[two][:].bitcast(I32), y[two][:].bitcast(I32), -1.0, float(RSQRT_MAGIC),
                                        ALU.mult, ALU.add).then_inc(seed_step, 1)

            def ip_front(m, mp, g, layer):
                two = (mp * G + g) % 2
                r = m - B
                c = 5 * (G * r + g)
                dve.wait_ge(dotn_done, G * r + g + 1)
                dve.wait_ge(att_done, 10 * r + 2 * g + 2)
                for t in range(NT):
                    last = nc.vector.scalar_tensor_tensor(out=fused[:, t], in0=att[:, g, t], scalar=SCALE, in1=dot[two][:, :, t, :],
                                                          op0=ALU.mult, op1=ALU.add)
                last.then_inc(ip_step, 1)
                dve.wait_ge(ip_step, c + 1)
                nc.vector.tensor_reduce(ip_max[:], fused[:], AX.X, ALU.max).then_inc(ip_step, 1)
                dve.wait_ge(ip_step, c + 2)
                nc.vector.tensor_tensor(fused[:], fused[:], ip_max[:].unsqueeze(3).to_broadcast([P, NT, HG, N_IP]),
                                        ALU.subtract).then_inc(ip_step, 1)

            def ip_back(m, mp, g, layer):
                r = m - B
                c = 5 * (G * r + g)
                k = 2 * (G * r + g)
                dve.wait_ge(ip_exp, G * r + g + 1)
                nc.vector.tensor_reduce(ip_den[:], fused[:], AX.X, ALU.add).then_inc(ip_step, 1)
                dve.wait_ge(ip_step, c + 4)
                nc.vector.reciprocal(ip_den[:], ip_den[:]).then_inc(ip_step, 1)
                dve.wait_ge(ip_step, c + 5)
                nc.vector.tensor_tensor(ip_den[:], ip_den[:], mask_c[:].unsqueeze(2).to_broadcast([P, NT, HG]),
                                        ALU.mult).then_inc(pip_done, 1)
                dve.wait_ge(pip_done, k + 1)
                if not first(r, g):
                    dve.wait_ge(it_ready, G * r + g)
                nc.vector.tensor_tensor(pip[:, :, WIN:WIN_IP].rearrange("p t (h n) -> p t h n", n=N_IP), fused[:],
                                        ip_den[:].unsqueeze(3).to_broadcast([P, NT, HG, N_IP]),
                                        ALU.mult).then_inc(pip_done, 1)

            def half(n, par, cur, prev, nxt):
                has_cur, has_prev, more = cur is not None, prev is not None, nxt is not None
                for slot in range(SLOTS):
                    a = (n, par, cur, prev, slot)
                    ipu = ip_pv_unit(*a)
                    if u := of(*a, lag=5, count=2 * G, layers=(1,)):
                        context_norm(*u, 1)
                    if u := norm_unit(*a):
                        norm_seed(*u)
                    su = s_unit(*a)
                    if su:
                        softmax_front(*su)
                    if not ipu and (u := pv_unit(*a)):
                        split_o_lo(*u)
                    if su:
                        key_sums(*su)
                    if u := of(*a, lag=4, count=2 * G, layers=(1,)):
                        context_norm(*u, 0)
                    if su:
                        key_sums_inverse(*su)
                    if ipu:
                        split_o_lo(*ipu)
                    if v := norm_unit(*a):
                        ip_front(*v)
                    if slot < G and has_cur:
                        dve.wait_ge(q_hi, G * n + slot + 1)
                        nc.vector.tensor_tensor(q_hl[:, 1, slot, :], proj_ps[slot % 2][:], q_hl[:, 0, slot, :].bitcast(F32),
                                                ALU.subtract).then_inc(q_lo, 1)
                    if slot >= G and has_prev:
                        m, mp, c = n - 1, 1 - par, slot - G
                        ring = (mp * G + c) % 2
                        dve.wait_ge(op_ready, G * m + c + 1)
                        if has_cur:
                            bank, residual, y_to = proj_ps[slot % 2][:], res[ring][:], outs[ring][:]
                            dve.wait_ge(res_in[ring], ring_count(m, mp, c))
                            if not (isinstance(m, int) and m == 0 and c < 2):
                                dve.wait_ge(out_done[ring], ring_count(m, mp, c) - 16)
                        else:
                            bank, residual, y_to = tail_banks[c], tail_res[c], tail_outs[c]
                            dve.wait_ge(tail_in, 16 * KC)
                        if isinstance(m, int) and m == 0 and c == 0:
                            dve.wait_ge(small_in, 16 * 3)
                        nc.vector.scalar_tensor_tensor(out=y_to, in0=bank, scalar=bias_c[:, prev, c:c + 1], in1=residual,
                                                       op0=ALU.add, op1=ALU.add).then_inc(y_out, 1)
                    if v := norm_unit(*a):
                        ip_back(*v)

            schedule(dve, half)

        @block.tensor
        def _(pe):

            def scores(m, mp, i, layer):
                g, tp = divmod(i, 2)
                c = 10 * m + i
                pe.wait_ge(q_lo, G * m + g + 1)
                if tp == 0:
                    pe.wait_ge(key_in[g], 16 * HG * (m + 1))
                if layer == 1 and not first(m - B, i):
                    pe.wait_ge(att_done, c - 10 * B)
                elif not first(m, i):
                    pe.wait_ge(sub_done, c)
                for b in range(2):
                    t = 2 * tp + b
                    for a, w in PASSES:
                        mm = nc.tensor.matmul(s_ps[:, b, 0:GL], q_hl[:, a, g, t * P:(t + 1) * P], key_bd[:, w, g, :],
                                              start=(a == w == 0), stop=(a == 1))
                mm.then_inc(s_ready, 1)

            def transposes(m, mp, i, layer):
                g, hp = divmod(i, 2)
                c = 10 * m + i
                if hp == 0:
                    pe.wait_ge(prob_done, 10 * m + 2 * g + 2)
                    if isinstance(m, int) and m == B:
                        pe.wait_ge(ones_set, g + 1 if g < 2 else G)
                if not (isinstance(m, int) and c == 0):
                    pe.wait_ge(t_copied, c)
                if first(m, i):
                    pe.wait_ge(consts, 4)
                for hh in range(2):
                    for t in range(NT):
                        at = t * GL + (2 * hp + hh) * L
                        mm = nc.tensor.transpose(t_ps[0:WIN, hh, t * P:(t + 1) * P], e[:, g, at:at + WIN], ident[:])
                mm.then_inc(t_ready, 1)

            def gram_product(m, mp, i, layer, hh):
                g, hp = divmod(i, 2)
                r = m - B
                c = 20 * r + 2 * i + hh
                if hh == 0:
                    pe.wait_ge(t_copied, 10 * m + i + 1)
                    if i == 0:
                        pe.wait_ge(gm_in, 16 * TEXT_DMAS * (r + 1))
                if not first(r, c):
                    pe.wait_ge(prod_done, c)
                buf = pT[(mp * G + g) % 2]
                for t in range(NT):
                    mm = nc.tensor.matmul(g_ps[:, t, :], buf[0:WIN, 2 * hp + hh, t * P:(t + 1) * P], gm[0:WIN, :],
                                          start=(t == 0), stop=(t == NT - 1), skip_group_check=True)
                mm.then_inc(g_ready, 1)

            def transpose_ip(m, mp, g, layer):
                pe.wait_ge(pip_done, 2 * (G * (m - B) + g) + 2)
                pe.wait_ge(o_lo, G * m + g)
                for t in range(NT):
                    mm = nc.tensor.transpose(o_ps[0:WIN_IP, t * P:(t + 1) * P], pip[:, t, :], ident[:])
                mm.then_inc(it_ready, 1)

            def values_product(m, mp, g, layer):
                pe.wait_ge(t_copied, 10 * m + 2 * g + 2)
                if g == 0:
                    pe.wait_ge(val_in, values_count(m, layer))
                if layer == 1:
                    if g == 0:
                        pe.wait_ge(valip_in, 16 * HG * (m - B + 1))
                    pe.wait_ge(it_copied, G * (m - B) + g + 1)
                elif not first(m, g):
                    pe.wait_ge(o_lo, G * m + g)
                buf = pT[(mp * G + g) % 2]
                rows = (WIN, WIN_IP)[layer]
                for h in range(HG):
                    at = g * P + h * D
                    mm = nc.tensor.matmul(o_ps[h * D:(h + 1) * D, :], val[0:rows, at:at + D], buf[0:rows, h, :],
                                          start=True, stop=True, tile_position=(0, h * D))
                mm.then_inc(pv_ready, 1)

            def project_tail(n, par, parts):
                for c, ks in parts:
                    pe.wait_ge(o_lo, G * (n - 1) + ks[-1] + 1)
                    if ks[0] == 0:
                        pe.wait_ge(w1_in[c], 32)
                        if c < 2:
                            pe.wait_ge(y_out, G * (n - 1))
                        elif c < 4:
                            pe.wait_ge(att_done, 10 * B)
                            pe.wait_ge(sub_done, 10 * n)
                        else:
                            pe.wait_ge(t_copied, 10 * n)
                    project(tail_banks[c], wo_hl, o_hl[1 - par], c, ks)

            def project(bank, w, rhs, c, ks):
                for k in ks:
                    for a, b in PASSES:
                        mm = nc.tensor.matmul(bank, w[:, a, k, c * P:(c + 1) * P], rhs[:, b, k, :],
                                              start=(k == 0 and a == b == 0), stop=(k == KC - 1 and a == 1))
                return mm

            def half(n, par, cur, prev, nxt):
                has_cur, has_prev, more = cur is not None, prev is not None, nxt is not None
                for slot in range(SLOTS):
                    a = (n, par, cur, prev, slot)
                    ipu = ip_pv_unit(*a)
                    if not ipu and (u := pv_unit(*a)):
                        values_product(*u)
                    tu = t_unit(*a)
                    gu = tu if tu and tu[3] == 1 else None
                    if tu:
                        transposes(*tu)
                    su = s_unit(*a)
                    q, o = slot < G and has_cur, slot >= G and has_prev and has_cur
                    bank = proj_ps[slot % 2][:]
                    if q:
                        if slot == 0:
                            if not first(n):
                                pe.wait_ge(x_lo, KC * n - 1)
                        if isinstance(n, int) and n == B:
                            pe.wait_ge(w1_in[slot], 16)
                        if slot == 1 and has_prev:
                            pe.wait_ge(sub_done, 10 * n)
                        if slot >= 2:
                            pe.wait_ge(q_lo, G * n + slot - 1)
                        args = (bank, wq_hl, x_hl, slot)
                        ready = qp_ready
                    elif o:
                        if slot == G:
                            pe.wait_ge(o_lo, G * n - prev)
                        if slot < G + 2:
                            if has_cur:
                                pe.wait_ge(q_lo, G * n + slot - 1)
                        else:
                            pe.wait_ge(y_out, G * (n - 1) + slot - G - 1)
                        if prev == 1:
                            pe.wait_ge(w1_in[slot - G], 32)
                        args = (bank, wo_hl, o_hl[1 - par], slot - G)
                        ready = op_ready
                    late_scores = su and su[2] == 0 and q
                    if su and not late_scores:
                        scores(*su)
                    if q or o:
                        project(*args, range(1))
                    if late_scores:
                        scores(*su)
                    if ipu:
                        transpose_ip(*ipu)
                    if q or o:
                        project(*args, range(1, 3))
                    if gu:
                        gram_product(*gu, 0)
                    if not has_cur:
                        project_tail(n, par, TAIL.get(slot, []))
                    if q or o:
                        project(*args, range(3, KC - 1))
                    if ipu:
                        values_product(*ipu)
                    if not has_cur and slot == G:
                        pe.wait_ge(o_lo, G * n)
                        for c in range(KC):
                            project(tail_banks[c], wo_hl, o_hl[1 - par], c, [KC - 1]).then_inc(op_ready, 1)
                    last_values = o and slot == G and prev == 1
                    if last_values:
                        if gu:
                            gram_product(*gu, 1)
                        pe.wait_ge(o_lo, G * n)
                    if q and slot == 0 and not first(n):
                        pe.wait_ge(x_lo, KC * n)
                    if q or o:
                        project(*args, range(KC - 1, KC)).then_inc(ready, 1)
                    if gu and not last_values:
                        gram_product(*gu, 1)

            schedule(pe, half)


def kernel(**inputs):
    import numpy as np
    import concourse.bacc as bacc
    from concourse.bass_utils import run_bass_kernel_spmd

    a = {k: np.asarray(v) for k, v in inputs.items()}
    arrays = {
        "xT": a["x"].transpose(0, 2, 1),
        "ctxT": a["ctx_2048"].reshape(TOK, E_CTX).T,
        "mask": a["fside_S_0"].reshape(NT, P).T,
        "L0_WqT": a["L0_xattn_Wq"].T,
        "L0_WkT": a["L0_xattn_Wk"].T,
        "L0_WvT": a["L0_xattn_Wv"].T,
        "L0_WoT": a["L0_xattn_Wo"].T,
        "L0_bo": a["L0_xattn_bo"].reshape(KC, P).T,
        "L1_Wq": a["L1_xattn_W_q"],
        "L1_Wk": a["L1_xattn_W_k"],
        "L1_Wv": a["L1_xattn_W_v"],
        "L1_Wkip": a["L1_xattn_W_k_ip"],
        "L1_Wvip": a["L1_xattn_W_v_ip"],
        "L1_Wo": a["L1_xattn_W_out"],
        "L1_bo": a["L1_xattn_b_out"].reshape(KC, P).T,
    }
    arrays = {k: np.ascontiguousarray(v) for k, v in arrays.items()}
    nc = bacc.Bacc("TRN2", target_bir_lowering=False, num_devices=1)
    args = {k: nc.dram_tensor(k, v.shape, mybir.dt.from_np(v.dtype), kind="ExternalInput").ap() for k, v in arrays.items()}
    out = nc.dram_tensor("outT", (B, C, S), F32, kind="ExternalOutput").ap()
    program(nc, outT=out, **args)
    r = run_bass_kernel_spmd(nc, [arrays], core_ids=[0])
    return r.results[0]["outT"].transpose(0, 2, 1)
```
